# Optimizing a Trainium2 kernel written in Bass

```python
import numpy as np
import jax
import jax.numpy as jnp

def _softmax(x, axis=-1):
    return jax.nn.softmax(x, axis=axis)

def _gelu(x):
    return jax.nn.gelu(x, approximate=True)

def _silu(x):
    return jax.nn.silu(x)

def _sigmoid(x):
    return jax.nn.sigmoid(x)

def _layernorm(x, axis=-1, eps=1e-05):
    m = jnp.mean(x, axis=axis, keepdims=True)
    v = jnp.var(x, axis=axis, keepdims=True)
    return (x - m) / jnp.sqrt(v + eps)

def _scatter_add(tgt, idx, src, axis=0):
    return tgt.at[idx].add(src)

def _segment_sum(src, seg, n):
    return jax.ops.segment_sum(src, seg, n)
kernel_name = 'mk_adj_preln_d2_adj_r2_d24bcc'

def setup_inputs(seed: int=0):
    np.random.seed(seed)
    _w = jnp.asarray

    def _rec_inputs():
        import jax
        import jax.numpy as jnp
        _gk = jax.random.key(seed)
        x = -0.000929 + 1 * jax.random.normal(jax.random.fold_in(_gk, 1), (8192, 64), jnp.float32)
        _a = jax.random.bernoulli(jax.random.fold_in(_gk, 2), 0.000976562, (8192, 8192))
        _a = jnp.logical_or(_a, jnp.eye(8192, dtype=bool))
        _af = _a.astype(jnp.float32)
        _af = _af * jax.random.uniform(jax.random.fold_in(_gk, 3), (8192, 8192), jnp.float32, 0.05, 1)
        adj = _af
        return (x, adj)
    x, adj = _rec_inputs()

    def _L0_gnn_setup():
        import jax, jax.numpy as jnp
        import numpy as np
        P_DROP = 0.1
        key = jax.random.key(seed)
        k1, k2, k3 = jax.random.split(key, 3)
        N, D = (8192, 64)
        x = jax.random.normal(k1, (N, D), dtype=jnp.float32)
        adj = jax.random.uniform(k2, (N, N), dtype=jnp.float32)
        u = jax.random.uniform(k3, (N, D), dtype=jnp.float32)
        return {'x': x, 'adj': adj, 'u': u}
    _L0_gnn_all = _L0_gnn_setup()
    _L0_gnn_in = {k: v for k, v in _L0_gnn_all.items() if k in ('u',)}
    del _L0_gnn_all

    def _L1_gnn_setup():
        import jax, jax.numpy as jnp
        import numpy as np
        HOP = 2
        N = 8192
        HIDDEN = 64
        key = jax.random.key(seed)
        k1, k2, k3 = jax.random.split(key, 3)
        user_embs = jax.random.normal(k1, (N, HIDDEN), dtype=jnp.float32)
        adj = jax.random.uniform(k2, (N, N), dtype=jnp.float32)
        limit = float(np.sqrt(6.0 / (2 * HIDDEN + HIDDEN)))
        W = jax.random.uniform(k3, (HOP, 2 * HIDDEN, HIDDEN), dtype=jnp.float32, minval=-limit, maxval=limit)
        return {'user_embs': user_embs, 'adj': adj, 'W': W}
    _L1_gnn_all = _L1_gnn_setup()
    _L1_gnn_in = {k: v for k, v in _L1_gnn_all.items() if k in ('W',)}
    del _L1_gnn_all
    return {'x': x, 'adj': adj, 'L0_gnn_u': _L0_gnn_in['u'], 'L1_gnn_W': _L1_gnn_in['W']}

def reference(x, adj, L0_gnn_u, L1_gnn_W):
    import jax
    import jax.numpy as jnp

    def _L0_gnn_ref(x, adj, u):
        import jax, jax.numpy as jnp
        import numpy as np
        P_DROP = 0.1
        keep = (u >= P_DROP).astype(x.dtype)
        x_drop = x * keep / (1.0 - P_DROP)
        return jnp.matmul(adj, x_drop)

    def _L1_gnn_ref(user_embs, adj, W):
        import jax, jax.numpy as jnp
        import numpy as np
        HOP = 2
        N = 8192
        HIDDEN = 64
        x = user_embs
        for k in range(HOP):
            agg = adj @ x
            x = jnp.tanh(jnp.concatenate([agg, x], axis=1) @ W[k])
        return x
    h = jnp.maximum(_layernorm(x, axis=-1), 0.0)
    x = x + _L0_gnn_ref(h, adj, L0_gnn_u)
    h = jnp.maximum(_layernorm(x, axis=-1), 0.0)
    x = x + _L1_gnn_ref(h, adj, L1_gnn_W)
    return x

_drawn_inputs = setup_inputs


def setup_inputs(seed=0):
    import zlib

    import numpy as np

    out = dict(_drawn_inputs(seed))
    spreads = {}
    factors = {}
    for name, (base, spread) in spreads.items():
        noise = np.random.default_rng([zlib.crc32(name.encode()), seed]).standard_normal(out[name].shape)
        drawn = base * np.exp(spread * noise) if base else spread * noise
        out[name] = jnp.asarray(drawn.astype(out[name].dtype))
    for name, factor in factors.items():
        out[name] = (out[name] * factor).astype(out[name].dtype)
    return out
```

```python
from contextlib import ExitStack

import numpy as np
import concourse.bass as bass
from concourse import mybir

N, D = 8192, 64
P = 128
BLK = 512
NB = N // BLK
Q = BLK // P
KT = N // P
SLOTS = 8
USES = NB // SLOTS
EPS = 1e-5
P_DROP = 0.1
PRE = 4
PT = KT // PRE

F32 = mybir.dt.float32
BF16 = mybir.dt.bfloat16
ALU = mybir.AluOpType
ACT = mybir.ActivationFunctionType
AX = mybir.AxisListType


def gnn_program(nc, adj, x, u, w, w_row, eye, out):
    with ExitStack() as ctx:
        def sb(name, shape, dt=F32):
            return ctx.enter_context(nc.sbuf_tensor(name, shape, dt))

        def bank(name, shape):
            return ctx.enter_context(nc.psum_tensor(name, shape, F32))

        def sem(name):
            return ctx.enter_context(nc.semaphore(name))

        ring = sb("ring", [P, SLOTS, Q * BLK])
        diag = sb("diag", [P, 2, Q * BLK])
        H = sb("H", [P, KT, 2 * D])
        X = sb("X", [P, KT, D])
        part = sb("part", [P, NB + 1, BLK])
        U_ = sb("U_", [P, PT * D])
        sq = sb("sq", [P, PT * D])
        cat = sb("cat", [P, BLK])
        fus = sb("fus", [P, BLK])
        hT = sb("hT", [D, BLK])
        hs = sb("hs", [P, Q, D])
        h2s = sb("h2s", [P, Q, D])
        xs = sb("xs", [P, Q, D])
        os_ = sb("os_", [P, Q, D])
        ident = sb("ident", [P, P])
        eye2 = sb("eye2", [P, D])
        wa = sb("wa", [P, 2, D])
        wb = sb("wb", [D, 2, D])
        zeros = sb("zeros", [P, BLK], BF16)
        epsb = sb("epsb", [P, 1])
        st = sb("st", [P, 8, KT])

        psU = bank("psU", [P, BLK])
        psF = bank("psF", [P, BLK])
        psD1 = bank("psD1", [P, BLK])
        psD3 = bank("psD3", [P, BLK])
        psT = bank("psT", [D, BLK])
        psZ = bank("psZ", [P, Q * D])

        slot_full = [sem(f"slot_full{k}") for k in range(SLOTS)]
        slot_free = [sem(f"slot_free{k}") for k in range(SLOTS)]
        diag_full, consts = sem("diag_full"), sem("consts")
        x_in = [sem(f"x_in{k}") for k in range(PRE)]
        u_in = [sem(f"u_in{k}") for k in range(PRE)]
        u_used, h0_ready, pre_var, pre_std = sem("u_used"), sem("h0_ready"), sem("pre_var"), sem("pre_std")
        zero_ready = sem("zero_ready")
        dchain, settled = sem("dchain"), sem("settled")
        a_done, a_u_out, a_f_out, a_part, a_xp = sem("a_done"), sem("a_u_out"), sem("a_f_out"), sem("a_part"), sem("a_xp")
        a_var, a_std, a_x1, a_h1 = sem("a_var"), sem("a_std"), sem("a_x1"), sem("a_h1")
        b_hs, b_d1, b_T, b_hT, b_cat0, b_done, b_cat, b_fout = [sem(n) for n in (
            "b_hs", "b_d1", "b_T", "b_hT", "b_cat0", "b_done", "b_cat", "b_fout")]
        b_z, b_h2s, b_h2, b_d3, b_d3out = [sem(n) for n in ("b_z", "b_h2s", "b_h2", "b_d3", "b_d3out")]
        c_hs, c_T, c_hT, c_done, c_cat, c_z, c_th, c_o, c_out, c_os = [sem(n) for n in (
            "c_hs", "c_T", "c_hT", "c_done", "c_cat", "c_z", "c_th", "c_o", "c_out", "c_os")]

        block = ctx.enter_context(nc.Block())

        def settle(eng):
            eng.sem_inc(settled, 1)

        def slot(s):
            return ring[:, s % SLOTS, :]

        @block.sync
        def _(sp):
            for k in range(PRE):
                sp.dma_start(X[:, k * PT:(k + 1) * PT, :],
                             x[:, k * PT * D:(k + 1) * PT * D]).then_inc(x_in[k], 16)
                if k >= 1:
                    sp.wait_ge(u_used, k)
                sp.dma_start(U_[:, :], u[:, k * PT * D:(k + 1) * PT * D]).then_inc(u_in[k], 16)
                if k == 0:
                    for s in range(SLOTS):
                        sp.dma_start(slot(s), adj[s]).then_inc(slot_full[s], 16)
            for s in range(SLOTS, NB):
                sp.wait_ge(slot_free[s % SLOTS], s // SLOTS)
                sp.dma_start(slot(s), adj[s]).then_inc(slot_full[s % SLOTS], 16)
            with sp.Fori(1, NB) as i:
                for s in range(NB):
                    sp.wait_ge(slot_free[s % SLOTS], USES * i + s // SLOTS)
                    sp.dma_start(slot(s), adj[i * NB + s]).then_inc(slot_full[s % SLOTS], 16)
            with sp.Fori(0, NB) as t:
                for s in range(NB):
                    with sp.If(t < s + 1):
                        sp.wait_ge(slot_free[s % SLOTS], USES * (NB + t) + s // SLOTS)
                        sp.sem_inc(slot_full[s % SLOTS], 16)
                    with sp.Else():
                        sp.wait_ge(slot_free[s % SLOTS], USES * (NB + t) + s // SLOTS)
                        settle(sp)
                        sp.dma_start(slot(s), adj[NB * NB - 1 - s - t * NB]).then_inc(slot_full[s % SLOTS], 16)
            with sp.Fori(0, NB) as t:
                for s in range(NB):
                    with sp.If(t < NB - 1 - s):
                        sp.wait_ge(slot_free[s % SLOTS], USES * (2 * NB + t) + s // SLOTS)
                        settle(sp)
                        sp.dma_start(slot(s), adj[(NB - 1) * NB + s - t * NB]).then_inc(slot_full[s % SLOTS], 16)
                    with sp.Else():
                        sp.wait_ge(slot_free[s % SLOTS], USES * (2 * NB + t) + s // SLOTS)
                        sp.sem_inc(slot_full[s % SLOTS], 16)

        @block.tensor
        def _(pe):
            def open_bank(ps):
                nc.tensor.matmul(ps[:, :], zeros[:, 0:P], zeros[:, :], start=True, stop=False, skip_group_check=True)

            def one(ps, moving, h, start=False):
                for q in range(Q):
                    lo = D * (q % 2)
                    m = nc.tensor.matmul(ps[lo:lo + D, :], h(q), moving[:, q * BLK:(q + 1) * BLK],
                                         start=start and q < 2, stop=q >= Q - 2, skip_group_check=True)
                return m

            def two(ps, moving, h):
                for q in range(Q):
                    m = nc.tensor.matmul(ps[:, :], h(q), moving[:, q * BLK:(q + 1) * BLK],
                                         start=False, stop=q == Q - 1, skip_group_check=True)
                return m

            def left(j):
                return lambda q: H[:, Q * j + q, 0:D]

            def both(j):
                return lambda q: H[:, Q * j + q, :]

            def first_layer_rows():
                for q in range(Q):
                    c = slice(q * P, (q + 1) * P)
                    nc.tensor.matmul(psZ[:, q * D:(q + 1) * D], cat[:, c], eye2[:, :], start=True, stop=False)
                    m = nc.tensor.matmul(psZ[:, q * D:(q + 1) * D], fus[0:D, c], eye2[0:D, :], start=False, stop=True)
                m.then_inc(a_xp, 1)

            def transposes(src):
                for q in range(Q):
                    m = nc.tensor.transpose(psT[:, q * P:(q + 1) * P], src[:, q, :], ident[:, :])
                return m

            def weights(hop):
                for q in range(Q):
                    c = slice(q * P, (q + 1) * P)
                    nc.tensor.matmul(psZ[:, q * D:(q + 1) * D], cat[:, c], wa[:, hop, :], start=True, stop=False)
                    m = nc.tensor.matmul(psZ[:, q * D:(q + 1) * D], hT[:, c], wb[:, hop, :], start=False, stop=True)
                return m

            pe.wait_ge(zero_ready, 1)
            pe.wait_ge(consts, 16 * 6)

            def row_a(i, first):
                if not first:
                    pe.wait_ge(a_u_out, i)
                    pe.wait_ge(a_f_out, i)
                    pe.wait_ge(a_part, i)
                open_bank(psU)
                open_bank(psF)
                for s in range(NB):
                    if first:
                        if s % (NB // PRE) == 0:
                            pe.wait_ge(h0_ready, s // (NB // PRE) + 1)
                        pe.wait_ge(slot_full[s % SLOTS], 16 * (s // SLOTS + 1))
                        m = one(psU, slot(s), left(s))
                        m.then_inc(slot_free[s % SLOTS], 1)
                        continue
                    if s == 0:
                        first_layer_rows()
                    pe.wait_ge(slot_full[s % SLOTS], 16 * (USES * i + s // SLOTS + 1))
                    with pe.If(i < s + 1):
                        one(psU, slot(s), left(s)).then_inc(slot_free[s % SLOTS], 1)
                    with pe.Else():
                        pe.wait_ge(a_h1, s + 1)
                        two(psF, slot(s), both(s)).then_inc(slot_free[s % SLOTS], 1)
                nc.tensor.matmul(psU[:, 0:1], zeros[:, 0:P], zeros[:, 0:1], start=False, stop=True,
                                 skip_group_check=True).then_inc(a_done, 1)

            row_a(0, True)
            with pe.Fori(1, NB) as i:
                row_a(i, False)
            pe.wait_ge(a_u_out, NB)
            pe.wait_ge(a_f_out, NB)
            first_layer_rows()

            pe.sem_inc(b_T, 1)
            pe.wait_ge(diag_full, 32)
            pe.wait_ge(a_part, NB)
            with pe.Fori(0, NB) as t:
                pe.wait_ge(b_fout, t + 1)
                open_bank(psF)
                pe.wait_ge(b_hs, t + 1)
                pe.wait_ge(diag_full, 16 * (t + 1))
                pe.wait_ge(b_cat0, t + 1)
                with pe.If(t % 2 == 0):
                    one(psD1, diag[:, 0, :], lambda q: hs[:, q, :], start=True).then_inc(b_d1, 1)
                with pe.Else():
                    one(psD1, diag[:, 1, :], lambda q: hs[:, q, :], start=True).then_inc(b_d1, 1)
                transposes(hs).then_inc(b_T, 1)
                for s in range(NB):
                    pe.wait_ge(slot_full[s % SLOTS], 16 * (USES * (NB + t) + s // SLOTS + 1))
                    with pe.If(t < s + 1):
                        pe.sem_inc(slot_free[s % SLOTS], 1)
                    with pe.Else():
                        pe.wait_ge(b_h2, s + 2)
                        two(psF, slot(s), both(NB - 1 - s)).then_inc(slot_free[s % SLOTS], 1)
                nc.tensor.matmul(psF[:, 0:1], zeros[:, 0:P], zeros[:, 0:1], start=False, stop=True,
                                 skip_group_check=True).then_inc(b_done, 1)
                with pe.If(t < 1):
                    pe.sem_inc(b_d3, 1)
                with pe.Else():
                    pe.wait_ge(b_d3out, t)
                    with pe.If(t % 2 == 1):
                        one(psD3, diag[:, 0, :], lambda q: h2s[:, q, :], start=True).then_inc(b_d3, 1)
                    with pe.Else():
                        one(psD3, diag[:, 1, :], lambda q: h2s[:, q, :], start=True).then_inc(b_d3, 1)
                pe.wait_ge(b_cat, t + 1)
                pe.wait_ge(b_hT, t + 1)
                weights(0).then_inc(b_z, 1)
            pe.wait_ge(b_d3out, NB)
            pe.wait_ge(b_h2, NB + 1)
            one(psD3, diag[:, (NB - 1) % 2, :], lambda q: h2s[:, q, :], start=True).then_inc(b_d3, 1)

            with pe.Fori(0, NB) as t:
                pe.wait_ge(c_cat, t + 1)
                open_bank(psU)
                for s in range(NB):
                    pe.wait_ge(slot_full[s % SLOTS], 16 * (USES * (2 * NB + t) + s // SLOTS + 1))
                    with pe.If(t < NB - 1 - s):
                        pe.wait_ge(b_h2, NB + 1 - s)
                        one(psU, slot(s), left(s)).then_inc(slot_free[s % SLOTS], 1)
                    with pe.Else():
                        pe.sem_inc(slot_free[s % SLOTS], 1)
                nc.tensor.matmul(psU[:, 0:1], zeros[:, 0:P], zeros[:, 0:1], start=False, stop=True,
                                 skip_group_check=True).then_inc(c_done, 1)
                pe.wait_ge(c_hs, t + 1)
                settle(pe)
                transposes(hs).then_inc(c_T, 1)
                pe.wait_ge(c_cat, t + 2)
                pe.wait_ge(c_hT, t + 1)
                weights(1).then_inc(c_z, 1)

        @block.scalar
        def _(act):
            for k in range(PRE):
                act.wait_ge(pre_var, k + 1)
                nc.scalar.activation(st[:, 2, k * PT:(k + 1) * PT], st[:, 1, k * PT:(k + 1) * PT],
                                     ACT.Sqrt, bias=epsb[:, 0:1], scale=1.0 / D).then_inc(pre_std, 1)
            with act.Fori(0, NB) as i:
                act.wait_ge(a_done, i + 1)
                nc.scalar.activation(cat[:, :], psU[:, :], ACT.Copy).then_inc(a_u_out, 1)
                nc.scalar.activation(fus[0:D, :], psF[0:D, :], ACT.Copy).then_inc(a_f_out, 1)
                act.wait_ge(a_var, i + 1)
                nc.scalar.activation(st[:, 2, 0:Q], st[:, 1, 0:Q], ACT.Sqrt, bias=epsb[:, 0:1],
                                     scale=1.0 / D).then_inc(a_std, 1)
            act.wait_ge(a_xp, NB)
            act.sem_inc(b_cat0, 1)
            with act.Fori(0, NB) as t:
                act.wait_ge(b_T, t + 2)
                nc.scalar.activation(hT[:, :], psT[:, :], ACT.Copy).then_inc(b_hT, 1)
                act.wait_ge(b_d1, t + 1)
                nc.scalar.activation(cat[:, :], psD1[:, :], ACT.Copy).then_inc(b_cat0, 1)
                act.wait_ge(b_z, t + 1)
                act.wait_ge(b_h2, t + 1)
                act.wait_ge(b_d3, t + 1)
                nc.scalar.activation(h2s[:, :, :], psZ[:, :].rearrange("p (q d) -> p q d", d=D),
                                     ACT.Tanh).then_inc(b_h2s, 1)
            with act.Fori(0, NB) as t:
                act.wait_ge(c_T, t + 1)
                nc.scalar.activation(hT[:, :], psT[:, :], ACT.Copy).then_inc(c_hT, 1)
                act.wait_ge(c_z, t + 1)
                act.wait_ge(c_o, t + 1)
                nc.scalar.activation(xs[:, :, :], psZ[:, :].rearrange("p (q d) -> p q d", d=D),
                                     ACT.Tanh).then_inc(c_th, 1)

        @block.vector
        def _(dve):
            count = [0]

            def link(ins, base=0):
                count[0] += 1
                ins.then_inc(dchain, 1)
                dve.wait_ge(dchain, base + count[0])

            def norm(xin, xc, sq_, n, k0, base, var_sem, var_value, std_sem, h_out, last_sem):
                sum_, var, std, r, e, m = (st[:, j, k0:k0 + n] for j in range(6))
                wide = lambda a: a.unsqueeze(2).broadcast_to((P, n, D))
                link(nc.vector.tensor_reduce(sum_, xin, AX.X, ALU.add), base)
                link(nc.vector.tensor_scalar(m, sum_, 1.0 / D, None, ALU.mult), base)
                link(nc.vector.tensor_tensor(xc, xin, wide(m), ALU.subtract), base)
                link(nc.vector.tensor_tensor(sq_, xc, xc, ALU.mult), base)
                nc.vector.tensor_reduce(var, sq_, AX.X, ALU.add).then_inc(var_sem, 1)
                dve.wait_ge(std_sem, var_value)
                link(nc.vector.reciprocal(r, std), base)
                link(nc.vector.tensor_scalar(m, var, 1.0 / D, EPS, ALU.mult, ALU.add), base)
                link(nc.vector.tensor_tensor(e, r, r, ALU.mult), base)
                link(nc.vector.tensor_tensor(e, e, m, ALU.mult), base)
                link(nc.vector.tensor_scalar(e, e, -0.5, 1.5, ALU.mult, ALU.add), base)
                link(nc.vector.tensor_tensor(r, r, e, ALU.mult), base)
                return nc.vector.scalar_tensor_tensor(h_out, xc, 0.0, wide(r), ALU.max, ALU.mult)

            nc.vector.memset(zeros[:, :], 0.0).then_inc(zero_ready, 1)
            link(nc.vector.memset(epsb[:, :], EPS))
            link(nc.vector.memset(st[:, :, :], 0.0))
            for k in range(PRE):
                a, b = k * PT, (k + 1) * PT
                u3 = U_[:, :].rearrange("p (t d) -> p t d", d=D)
                s3 = sq[:, :].rearrange("p (t d) -> p t d", d=D)
                dve.wait_ge(x_in[k], 16)
                link(norm(X[:, a:b, :], H[:, a:b, 0:D], s3, PT, a, 0, pre_var, k + 1, pre_std, H[:, a:b, 0:D], None))
                dve.wait_ge(u_in[k], 16)
                link(nc.vector.tensor_scalar(s3, u3, float(np.float32(P_DROP)), float(np.float32(1.0) / np.float32(1.0 - P_DROP)),
                                             ALU.is_ge, ALU.mult))
                dve.sem_inc(u_used, 1)
                nc.vector.tensor_tensor(H[:, a:b, 0:D], H[:, a:b, 0:D], s3, ALU.mult).then_inc(h0_ready, 1)

            dve.wait_ge(h0_ready, PRE)
            base0 = count[0]
            per_row = 12
            with dve.Fori(0, NB) as i:
                count[0] = 0
                base = base0 + per_row * i
                dve.wait_ge(a_done, i + 1)
                nc.vector.tensor_copy(part[D:P, bass.ds(i, 1), :], psF[D:P, :].unsqueeze(1)).then_inc(a_part, 1)
                dve.wait_ge(a_xp, i + 1)
                rows = X[:, bass.ds(Q * i, Q), :]
                link(nc.vector.tensor_tensor(xs[:, :, :], psZ[:, :].rearrange("p (q d) -> p q d", d=D), rows, ALU.add), base)
                link(norm(xs[:, :, :], os_[:, :, :], h2s[:, :, :], Q, 0, base, a_var, i + 1, a_std,
                          H[:, bass.ds(Q * i, Q), D:2 * D], None), base)
                settle(dve)
                nc.vector.tensor_copy(rows, xs[:, :, :]).then_inc(a_h1, 1)
                assert count[0] == per_row
            base0 += per_row * NB

            dve.wait_ge(a_h1, NB)
            dve.sem_inc(b_fout, 1)
            dve.sem_inc(b_h2, 1)
            per_row = 2
            with dve.Fori(0, NB) as t:
                count[0] = 0
                base = base0 + per_row * t
                own = bass.ds(NB - 1 - t, 1)
                up = cat[D:P, :].unsqueeze(1)
                dve.wait_ge(b_cat0, t + 2)
                settle(dve)
                link(nc.vector.tensor_tensor(up, up, part[D:P, own, :], ALU.add), base)
                dve.wait_ge(b_done, t + 1)
                nc.vector.tensor_tensor(up, psF[D:P, :].unsqueeze(1), up, ALU.add).then_inc(b_cat, 1)
                link(nc.vector.tensor_copy(part[0:D, own, :], psF[0:D, :].unsqueeze(1)), base)
                dve.sem_inc(b_fout, 1)
                with dve.If(t < 1):
                    dve.sem_inc(b_d3out, 1)
                with dve.Else():
                    dve.wait_ge(b_d3, t + 1)
                    settle(dve)
                    below = bass.ds(NB - t, 1)
                    lo = part[0:D, below, :]
                    nc.vector.tensor_tensor(lo, psD3[0:D, :].unsqueeze(1), lo, ALU.add)
                    nc.vector.tensor_copy(part[D:P, below, :], psD3[D:P, :].unsqueeze(1)).then_inc(b_d3out, 1)
                dve.wait_ge(b_h2s, t + 1)
                nc.vector.tensor_copy(H[:, bass.ds(Q * (NB - 1) - Q * t, Q), 0:D], h2s[:, :, :]).then_inc(b_h2, 1)
                assert count[0] == per_row
            dve.wait_ge(b_d3, NB + 1)
            link(nc.vector.tensor_tensor(part[0:D, 0, :], psD3[0:D, :], part[0:D, 0, :], ALU.add), base0 + per_row * NB - per_row)
            link(nc.vector.tensor_copy(part[D:P, 0, :], psD3[D:P, :]), base0 + per_row * NB - per_row)
            dve.sem_inc(b_d3out, 1)

            dve.sem_inc(c_cat, 1)
            dve.sem_inc(c_o, 1)
            with dve.Fori(0, NB) as t:
                own = bass.ds(NB - 1 - t, 1)
                dve.wait_ge(c_done, t + 1)
                settle(dve)
                nc.vector.tensor_tensor(cat[:, :].unsqueeze(1), psU[:, :].unsqueeze(1), part[:, own, :], ALU.add).then_inc(c_cat, 1)
                dve.wait_ge(c_th, t + 1)
                dve.wait_ge(c_os, t + 1)
                nc.vector.tensor_tensor(os_[:, :, :], xs[:, :, :], X[:, bass.ds(Q * (NB - 1) - Q * t, Q), :],
                                        ALU.add).then_inc(c_o, 1)

        @block.gpsimd
        def _(pool):
            pool.dma_start(ident[:, :], eye).then_inc(consts, 16)
            pool.dma_start(eye2[0:D, :], eye[0:D, 0:D]).then_inc(consts, 16)
            pool.dma_start(eye2[D:P, :], eye[0:D, 0:D]).then_inc(consts, 16)
            pool.dma_start(wa[0:D, :, :], w[:, 0:D, :].rearrange("k r c -> r k c")).then_inc(consts, 16)
            pool.dma_start(wa[D:P, :, :], w[:, 0:D, :].rearrange("k r c -> r k c")).then_inc(consts, 16)
            pool.dma_start(wb[:, :, :], w[:, D:2 * D, :].rearrange("k r c -> r k c")).then_inc(consts, 16)
            for t in range(2):
                pool.dma_start(diag[:, t, :], adj[(NB - 1 - t) * (NB + 1)]).then_inc(diag_full, 16)
            pool.wait_ge(a_h1, NB)
            own = lambda t, lo: H[:, bass.ds(Q * (NB - 1) - Q * t, Q), lo:lo + D]
            nc.gpsimd.tensor_copy(hs[:, :, :], own(0, D)).then_inc(b_hs, 1)
            pool.wait_ge(b_T, 2)
            nc.gpsimd.tensor_copy(hs[:, :, :], own(1, D)).then_inc(b_hs, 1)
            with pool.Fori(1, NB - 1) as t:
                pool.wait_ge(b_T, t + 2)
                settle(pool)
                nc.gpsimd.tensor_copy(hs[:, :, :], own(t + 1, D)).then_inc(b_hs, 1)
                pool.wait_ge(b_d3, t + 1)
                settle(pool)
                with pool.If(t % 2 == 1):
                    pool.dma_start(diag[:, 0, :], adj[(NB - 2) * (NB + 1) - (NB + 1) * t]).then_inc(diag_full, 16)
                with pool.Else():
                    pool.dma_start(diag[:, 1, :], adj[(NB - 2) * (NB + 1) - (NB + 1) * t]).then_inc(diag_full, 16)
            pool.wait_ge(b_T, NB + 1)
            pool.sem_inc(c_os, 1)
            pool.wait_ge(b_h2, NB + 1)
            with pool.Fori(0, NB) as t:
                nc.gpsimd.tensor_copy(hs[:, :, :], H[:, bass.ds(Q * (NB - 1) - Q * t, Q), 0:D]).then_inc(c_hs, 1)
                pool.wait_ge(c_o, t + 2)
                settle(pool)
                pool.dma_start(out[NB - 1 - t], os_[:, :, :].rearrange("p q d -> p (q d)")).then_inc(c_out, 16)
                pool.wait_ge(c_out, 16 * (t + 1))
                pool.sem_inc(c_os, 1)
            pool.wait_ge(c_out, 16 * NB)


def kernel(x, adj, L0_gnn_u, L1_gnn_W):
    import concourse.bacc as bacc
    from concourse.bass_utils import run_bass_kernel_spmd

    def tiles(a):
        return np.ascontiguousarray(np.asarray(a).reshape(KT, P, D).transpose(1, 0, 2)).reshape(P, KT * D)

    blocks = np.asarray(adj).reshape(NB, BLK, NB, Q, P).transpose(0, 2, 4, 3, 1)
    arrays = {
        "adj": np.ascontiguousarray(blocks).reshape(NB * NB, P, Q * BLK),
        "x": tiles(x),
        "u": tiles(L0_gnn_u),
        "w": np.ascontiguousarray(L1_gnn_W),
        "eye": np.eye(P, dtype=np.float32),
    }
    nc = bacc.Bacc("TRN2", target_bir_lowering=False, num_devices=1)
    ins = {k: nc.dram_tensor(f"{k}_dram", a.shape, F32, kind="ExternalInput").ap() for k, a in arrays.items()}
    out = nc.dram_tensor("out_dram", (NB, P, Q * D), F32, kind="ExternalOutput").ap()
    gnn_program(nc, ins["adj"], ins["x"], ins["u"], ins["w"], None, ins["eye"], out)
    r = run_bass_kernel_spmd(nc, [{f"{k}_dram": a for k, a in arrays.items()}], core_ids=[0])
    got = r.results[0]["out_dram"]
    return np.asarray(got).reshape(NB, P, Q, D).transpose(0, 2, 1, 3).reshape(N, D)
```

```python
from contextlib import ExitStack

import numpy as np
import concourse.bass as bass
from concourse import mybir

N, D = 8192, 64
P = 128
BLK = 512
NB = N // BLK
Q = BLK // P
KT = N // P
SLOTS = 8
USES = NB // SLOTS
ITEMS = SLOTS // 2
SETS = NB // ITEMS
EPS = 1e-5
P_DROP = 0.1
PRE = 4
PT = KT // PRE

F32 = mybir.dt.float32
BF16 = mybir.dt.bfloat16
ALU = mybir.AluOpType
ACT = mybir.ActivationFunctionType
AX = mybir.AxisListType


def rows_in(a):
    return ITEMS if a < SETS - 1 else ITEMS - 1


def fours_before(a):
    return sum(rows_in(c) * (c + 1) for c in range(a))


ALL_FOURS = fours_before(SETS)


def gnn_program(nc, adj, x, u, w, eye, out):
    with ExitStack() as ctx:
        def sb(name, shape, dt=F32):
            return ctx.enter_context(nc.sbuf_tensor(name, shape, dt))

        def bank(name, shape):
            return ctx.enter_context(nc.psum_tensor(name, shape, F32))

        def sem(name):
            return ctx.enter_context(nc.semaphore(name))

        ring = sb("ring", [P, SLOTS, Q * BLK])
        diag = sb("diag", [P, 2, Q * BLK])
        H = sb("H", [P, KT, 2 * D])
        X = sb("X", [P, KT, D])
        part = sb("part", [P, NB + 1, BLK])
        U_ = sb("U_", [P, PT * D])
        sq = sb("sq", [P, PT * D])
        cat2 = sb("cat2", [P, 2, BLK])
        cat, fus = cat2[:, 0, :], cat2[:, 1, :]
        hT = sb("hT", [D, 2, BLK])
        hs = sb("hs", [P, Q, D])
        h2s = sb("h2s", [P, Q, D])
        xs = sb("xs", [P, Q, D])
        xc = sb("xc", [P, Q, D])
        col = sb("col", [P, Q, D])
        ident = sb("ident", [P, P])
        eye2 = sb("eye2", [P, D])
        wa = sb("wa", [P, 2, D])
        wb = sb("wb", [D, 2, D])
        zeros = sb("zeros", [P, BLK], BF16)
        epsb = sb("epsb", [P, 1])
        st = sb("st", [P, 8, KT])

        psU = bank("psU", [P, BLK])
        psF = bank("psF", [P, BLK])
        psV = bank("psV", [P, BLK])
        psD1 = bank("psD1", [P, BLK])
        psD3 = bank("psD3", [P, BLK])
        psT = bank("psT", [D, BLK])
        psZ = bank("psZ", [P, Q * D])

        slot_full = [sem(f"slot_full{k}") for k in range(SLOTS)]
        slot_free = [sem(f"slot_free{k}") for k in range(SLOTS)]
        diag_full, consts = sem("diag_full"), sem("consts")
        x_in = [sem(f"x_in{k}") for k in range(PRE)]
        u_in = [sem(f"u_in{k}") for k in range(PRE)]
        u_used, h0_ready, pre_var, pre_std = sem("u_used"), sem("h0_ready"), sem("pre_var"), sem("pre_std")
        zero_ready = sem("zero_ready")
        dchain, settled = sem("dchain"), sem("settled")
        a_done, a_u_out, a_f_out, a_part, a_xp = [sem(n) for n in ("a_done", "a_u_out", "a_f_out", "a_part", "a_xp")]
        a_var, a_std, a_x1, a_h1 = sem("a_var"), sem("a_std"), sem("a_x1"), sem("a_h1")
        b_hs, b_d1, b_T, b_hT, b_catlo, b_done, b_up, b_cat, b_fout = [sem(n) for n in (
            "b_hs", "b_d1", "b_T", "b_hT", "b_catlo", "b_done", "b_up", "b_cat", "b_fout")]
        b_z, b_h2s, b_h2, b_d3, b_d3out = [sem(n) for n in ("b_z", "b_h2s", "b_h2", "b_d3", "b_d3out")]
        b_col, b_under, b_added = sem("b_col"), sem("b_under"), sem("b_added")
        e_hs, e_T, e_hT, e_mm, e_cat, e_z, e_th, e_o, e_out = [sem(n) for n in (
            "e_hs", "e_T", "e_hT", "e_mm", "e_cat", "e_z", "e_th", "e_o", "e_out")]

        block = ctx.enter_context(nc.Block())

        def settle(eng):
            eng.sem_inc(settled, 1)

        def slot(s):
            return ring[:, s % SLOTS, :]

        def upper(eng, b, a, q, k, then, otherwise):
            if q < a or k == 0:
                return then()
            with eng.If(b > k - 1):
                then()
            with eng.Else():
                otherwise()

        def under(eng, b, a, q, k, then, otherwise):
            least = k + 2 - ITEMS * (a - q)
            if least <= 0:
                return then()
            if least >= rows_in(a):
                return otherwise()
            with eng.If(b > least - 1):
                then()
            with eng.Else():
                otherwise()

        def fours(a, b):
            return fours_before(a) + (a + 1) * b

        @block.sync
        def _(sp):
            for k in range(PRE):
                sp.dma_start(X[:, k * PT:(k + 1) * PT, :],
                             x[:, k * PT * D:(k + 1) * PT * D]).then_inc(x_in[k], 16)
                if k >= 1:
                    sp.wait_ge(u_used, k)
                sp.dma_start(U_[:, :], u[:, k * PT * D:(k + 1) * PT * D]).then_inc(u_in[k], 16)
                if k == 0:
                    for s in range(SLOTS):
                        sp.dma_start(slot(s), adj[s]).then_inc(slot_full[s], 16)
            for s in range(SLOTS, NB):
                sp.wait_ge(slot_free[s % SLOTS], s // SLOTS)
                sp.dma_start(slot(s), adj[s]).then_inc(slot_full[s % SLOTS], 16)
            with sp.Fori(1, NB) as i:
                for s in range(NB):
                    sp.wait_ge(slot_free[s % SLOTS], USES * i + s // SLOTS)
                    sp.dma_start(slot(s), adj[i * NB + s]).then_inc(slot_full[s % SLOTS], 16)
            def load(k, use, block):
                sp.wait_ge(slot_free[k], use)
                settle(sp)
                sp.dma_start(ring[:, k, :], block()).then_inc(slot_full[k], 16)

            def skip(k, use):
                sp.wait_ge(slot_free[k], use)
                sp.sem_inc(slot_full[k], 16)

            sp.dma_start(diag[:, 0, :], adj[NB * NB - 1]).then_inc(diag_full, 16)
            for a in range(SETS):
                with sp.Fori(0, rows_in(a)) as b:
                    for q in range(a + 1):
                        use = USES * NB + fours(a, b) + q
                        for k in range(ITEMS):
                            s = ITEMS * q + k
                            upper(sp, b, a, q, k,
                                  lambda: load(2 * k, use, lambda: adj[NB * NB - 1 - s - NB * (ITEMS * a + 1) - NB * b]),
                                  lambda: skip(2 * k, use))
                            under(sp, b, a, q, k,
                                  lambda: load(2 * k + 1, use, lambda: adj[nc.s_assert_within(
                                      NB * (NB - 1 - s) + NB - ITEMS * a - b, 0, NB * NB - 1,
                                      skip_runtime_bounds_check_because="only rows with b > 0 get here where a is 0")]),
                                  lambda: skip(2 * k + 1, use))
                    sp.wait_ge(b_d3, ITEMS * a + 1 + b)
                    settle(sp)
                    where = NB * NB - 1 - (NB + 1) * (ITEMS * a + 1) - (NB + 1) * b
                    with sp.If(b % 2 == 0):
                        sp.dma_start(diag[:, 1, :], adj[where]).then_inc(diag_full, 16)
                    with sp.Else():
                        sp.dma_start(diag[:, 0, :], adj[where]).then_inc(diag_full, 16)

            def load_tail(r, j, use, row):
                load((2 * r + j) % SLOTS, use, lambda: adj[NB * row + 1 - j])

            base = USES * NB + ALL_FOURS
            for j in range(2):
                load_tail(0, j, base, NB - 1)
            with sp.Fori(0, 3) as c:
                for k in range(ITEMS):
                    for j in range(2):
                        load_tail(1 + k, j, base + (1 + k) // ITEMS + c, NB - 2 - k - ITEMS * c)
            for j in range(2):
                load_tail(13, j, base + 3, 2)
            sp.wait_ge(slot_free[4], base + 3)
            sp.dma_start(ring[:, 4, :], adj[NB]).then_inc(slot_full[4], 16)

        @block.tensor
        def _(pe):
            def open_bank(ps):
                nc.tensor.matmul(ps[:, :], zeros[:, 0:P], zeros[:, :], start=True, stop=False, skip_group_check=True)

            def one(ps, moving, h, start=False):
                for q in range(Q):
                    lo = D * (q % 2)
                    m = nc.tensor.matmul(ps[lo:lo + D, :], h(q), moving[:, q * BLK:(q + 1) * BLK],
                                         start=start and q < 2, stop=q >= Q - 2, skip_group_check=True)
                return m

            def two(ps, moving, h):
                for q in range(Q):
                    m = nc.tensor.matmul(ps[:, :], h(q), moving[:, q * BLK:(q + 1) * BLK],
                                         start=False, stop=q == Q - 1, skip_group_check=True)
                return m

            def left(j):
                return lambda q: H[:, Q * j + q, 0:D]

            def both(j):
                return lambda q: H[:, Q * j + q, :]

            def first_layer_rows():
                for q in range(Q):
                    c = slice(q * P, (q + 1) * P)
                    nc.tensor.matmul(psZ[:, q * D:(q + 1) * D], cat[:, c], eye2[:, :], start=True, stop=False)
                    m = nc.tensor.matmul(psZ[:, q * D:(q + 1) * D], fus[0:D, c], eye2[0:D, :], start=False, stop=True)
                m.then_inc(a_xp, 1)

            def transposes(src):
                for q in range(Q):
                    m = nc.tensor.transpose(psT[:, q * P:(q + 1) * P], src[:, q, :], ident[:, :])
                return m

            def weights(hop, cat=cat, hT=hT[:, 0, :]):
                for q in range(Q):
                    c = slice(q * P, (q + 1) * P)
                    nc.tensor.matmul(psZ[:, q * D:(q + 1) * D], cat[:, c], wa[:, hop, :], start=True, stop=False)
                    m = nc.tensor.matmul(psZ[:, q * D:(q + 1) * D], hT[:, c], wb[:, hop, :], start=False, stop=True)
                return m

            pe.wait_ge(zero_ready, 1)
            pe.wait_ge(consts, 16 * 6)

            def row_a(i, first):
                if not first:
                    pe.wait_ge(a_u_out, i)
                    pe.wait_ge(a_f_out, i)
                open_bank(psU)
                open_bank(psF)
                for s in range(NB):
                    if first:
                        if s % (NB // PRE) == 0:
                            pe.wait_ge(h0_ready, s // (NB // PRE) + 1)
                        pe.wait_ge(slot_full[s % SLOTS], 16 * (s // SLOTS + 1))
                        m = one(psU, slot(s), left(s))
                        m.then_inc(slot_free[s % SLOTS], 1)
                        continue
                    if s == 0:
                        first_layer_rows()
                    pe.wait_ge(slot_full[s % SLOTS], 16 * (USES * i + s // SLOTS + 1))
                    with pe.If(i < s + 1):
                        one(psU, slot(s), left(s)).then_inc(slot_free[s % SLOTS], 1)
                    with pe.Else():
                        pe.wait_ge(a_h1, s + 1)
                        two(psF, slot(s), both(s)).then_inc(slot_free[s % SLOTS], 1)
                nc.tensor.matmul(psU[:, 0:1], zeros[:, 0:P], zeros[:, 0:1], start=False, stop=True,
                                 skip_group_check=True).then_inc(a_done, 1)

            row_a(0, True)
            with pe.Fori(1, NB) as i:
                row_a(i, False)
            pe.wait_ge(a_u_out, NB)
            pe.wait_ge(a_f_out, NB)
            first_layer_rows()

            fixed = lambda h: lambda q: h[:, q, :]

            def row_b(t, a=None, b=None):
                pe.wait_ge(b_fout, t + 1)
                open_bank(psF)
                pe.wait_ge(b_hs, t + 1)
                settle(pe)
                transposes(hs).then_inc(b_T, 1)
                for q in range(0 if a is None else a + 1):
                    use = USES * NB + fours(a, b) + q
                    for k in range(ITEMS):
                        s = ITEMS * q + k
                        item = ITEMS * (fours(a, b) + q) + k

                        def pass_slot(m):
                            pe.wait_ge(slot_full[m], 16 * use + 16)
                            pe.sem_inc(slot_free[m], 1)

                        def right():
                            pe.wait_ge(slot_full[2 * k], 16 * use + 16)
                            pe.wait_ge(b_h2, s + 2)
                            two(psF, ring[:, 2 * k, :], both(NB - 1 - s)).then_inc(slot_free[2 * k], 1)

                        def below():
                            if k == 0:
                                pe.wait_ge(b_col, t)
                            pe.wait_ge(slot_full[2 * k + 1], 16 * use + 16)
                            pe.wait_ge(b_added, item + 1)
                            m = one((psU, psV)[k % 2], ring[:, 2 * k + 1, :], fixed(col), start=True)
                            m.then_inc(slot_free[2 * k + 1], 1)
                            nc.tensor.matmul((psU, psV)[k % 2][:, 0:1], zeros[:, 0:P], zeros[:, 0:1], start=False, stop=True,
                                             skip_group_check=True).then_inc(b_under, 1)

                        def none_below():
                            pe.wait_ge(b_added, item + 2)
                            pe.sem_inc(b_under, 1)
                            pass_slot(2 * k + 1)

                        upper(pe, b, a, q, k, right, lambda: pass_slot(2 * k))
                        under(pe, b, a, q, k, below, none_below)
                nc.tensor.matmul(psF[:, 0:1], zeros[:, 0:P], zeros[:, 0:1], start=False, stop=True,
                                 skip_group_check=True).then_inc(b_done, 1)
                pe.wait_ge(diag_full, 16 * t + 16)
                if a is None:
                    one(psD1, diag[:, 0, :], fixed(hs), start=True).then_inc(b_d1, 1)
                    pe.sem_inc(b_d3, 1)
                else:
                    for last, (ps, h, there) in enumerate(((psD1, hs, b_d1), (psD3, h2s, b_d3))):
                        if last:
                            pe.wait_ge(b_d3out, t)
                            pe.wait_ge(b_h2, t + 1)
                        with pe.If(b % 2 == 0):
                            one(ps, diag[:, 1 - last, :], fixed(h), start=True).then_inc(there, 1)
                        with pe.Else():
                            one(ps, diag[:, last, :], fixed(h), start=True).then_inc(there, 1)
                pe.wait_ge(b_cat, t + 1)
                pe.wait_ge(b_catlo, t + 1)
                pe.wait_ge(b_hT, t + 1)
                weights(0).then_inc(b_z, 1)

            row_b(0)
            for a in range(SETS):
                with pe.Fori(0, rows_in(a)) as b:
                    row_b(b + ITEMS * a + 1, a, b)

            base = USES * NB + ALL_FOURS

            def row_tail(r, k, use):
                ps = (psU, psV)[k % 2]
                for j in range(2):
                    m = (2 * k + j) % SLOTS
                    pe.wait_ge(slot_full[m], 16 * use + 16)
                    if j == 0:
                        pe.wait_ge(e_cat, r + 1)
                    else:
                        pe.wait_ge(b_h2, NB + 1)
                    for q in range(Q):
                        lo = D * (q % 2)
                        x = nc.tensor.matmul(ps[lo:lo + D, :], left(1 - j)(q), ring[:, m, q * BLK:(q + 1) * BLK],
                                             start=j == 0 and q < 2, stop=j == 1 and q >= 2, skip_group_check=True)
                    x.then_inc(slot_free[m], 1)
                nc.tensor.matmul(ps[:, 0:1], zeros[:, 0:P], zeros[:, 0:1], start=False, stop=True,
                                 skip_group_check=True).then_inc(e_mm, 1)

            def turn_tail(r):
                pe.wait_ge(e_hT, r + 1)
                pe.wait_ge(e_hs, r + 1)
                settle(pe)
                transposes(hs).then_inc(e_T, 1)

            def out_tail(r, k):
                pe.wait_ge(e_cat, r + 3)
                pe.wait_ge(e_hT, r + 2)
                pe.wait_ge(e_th, r + 1)
                settle(pe)
                weights(1, cat2[:, k % 2, :], hT[:, k % 2, :]).then_inc(e_z, 1)

            pe.sem_inc(e_T, 1)
            row_tail(0, 0, base)
            turn_tail(0)
            pe.wait_ge(b_d3out, NB)
            one(psD3, diag[:, (NB - 1) % 2, :], fixed(h2s), start=True).then_inc(b_d3, 1)
            with pe.Fori(0, 3) as c:
                for k in range(1, 1 + ITEMS):
                    r = ITEMS * c + k
                    row_tail(r, k, c + base + k // ITEMS)
                    turn_tail(r)
                    out_tail(r - 1, k - 1)
            row_tail(13, 1, base + 3)
            turn_tail(13)
            out_tail(12, 0)
            pe.wait_ge(slot_full[4], 16 * (base + 4))
            pe.wait_ge(e_cat, 14 + 1)
            one(psU, ring[:, 4, :], left(0), start=True).then_inc(slot_free[4], 1)
            nc.tensor.matmul(psU[:, 0:1], zeros[:, 0:P], zeros[:, 0:1], start=False, stop=True,
                             skip_group_check=True).then_inc(e_mm, 1)
            turn_tail(14)
            out_tail(13, 1)
            turn_tail(15)
            out_tail(14, 0)
            out_tail(15, 1)

        @block.scalar
        def _(act):
            act.dma_start(ident[:, :], eye).then_inc(consts, 16)
            act.dma_start(eye2[0:D, :], eye[0:D, 0:D]).then_inc(consts, 16)
            act.dma_start(eye2[D:P, :], eye[0:D, 0:D]).then_inc(consts, 16)
            act.dma_start(wa[0:D, :, :], w[:, 0:D, :].rearrange("k r c -> r k c")).then_inc(consts, 16)
            act.dma_start(wa[D:P, :, :], w[:, 0:D, :].rearrange("k r c -> r k c")).then_inc(consts, 16)
            act.dma_start(wb[:, :, :], w[:, D:2 * D, :].rearrange("k r c -> r k c")).then_inc(consts, 16)
            for k in range(PRE):
                act.wait_ge(pre_var, k + 1)
                nc.scalar.activation(st[:, 2, k * PT:(k + 1) * PT], st[:, 1, k * PT:(k + 1) * PT],
                                     ACT.Sqrt, bias=epsb[:, 0:1], scale=1.0 / D).then_inc(pre_std, 1)
            with act.Fori(0, NB) as i:
                act.wait_ge(a_done, i + 1)
                nc.scalar.activation(cat[:, :], psU[:, :], ACT.Copy).then_inc(a_u_out, 1)
                act.wait_ge(a_var, i + 1)
                nc.scalar.activation(st[:, 2, 0:Q], st[:, 1, 0:Q], ACT.Sqrt, bias=epsb[:, 0:1],
                                     scale=1.0 / D).then_inc(a_std, 1)
            act.wait_ge(a_xp, NB)

            def row_b(t):
                act.wait_ge(b_T, t + 1)
                nc.scalar.activation(hT[:, 0, :], psT[:, :], ACT.Copy).then_inc(b_hT, 1)
                act.wait_ge(b_d1, t + 1)
                nc.scalar.activation(cat[0:D, :], psD1[0:D, :], ACT.Copy).then_inc(b_catlo, 1)
                act.wait_ge(b_h2, t + 1)
                act.wait_ge(b_d3, t + 1)
                act.wait_ge(b_z, t + 1)
                nc.scalar.activation(h2s[:, :, :], psZ[:, :].rearrange("p (q d) -> p q d", d=D),
                                     ACT.Tanh).then_inc(b_h2s, 1)

            with act.Fori(0, NB) as t:
                row_b(t)

            def turn_tail(r, k):
                act.wait_ge(e_T, r + 2)
                nc.scalar.activation(hT[:, k % 2, :], psT[:, :], ACT.Copy).then_inc(e_hT, 1)

            def out_tail(r):
                act.wait_ge(e_o, r + 1)
                act.wait_ge(e_z, r + 1)
                nc.scalar.activation(xs[:, :, :], psZ[:, :].rearrange("p (q d) -> p q d", d=D),
                                     ACT.Tanh).then_inc(e_th, 1)

            act.sem_inc(e_hT, 1)
            act.sem_inc(e_th, 1)
            turn_tail(0, 0)
            with act.Fori(0, 7) as c:
                for k in range(1, 3):
                    r = 2 * c + k
                    turn_tail(r, k)
                    out_tail(r - 1)
            turn_tail(15, 1)
            out_tail(14)
            out_tail(15)

        @block.vector
        def _(dve):
            count = [0]

            def link(ins, base=0):
                count[0] += 1
                ins.then_inc(dchain, 1)
                dve.wait_ge(dchain, base + count[0])

            def norm(xin, xc, sq_, n, k0, base, var_sem, var_value, std_sem, h_out, last_sem):
                sum_, var, std, r, e, m = (st[:, j, k0:k0 + n] for j in range(6))
                wide = lambda a: a.unsqueeze(2).broadcast_to((P, n, D))
                link(nc.vector.tensor_reduce(sum_, xin, AX.X, ALU.add), base)
                link(nc.vector.tensor_scalar(m, sum_, 1.0 / D, None, ALU.mult), base)
                link(nc.vector.tensor_tensor(xc, xin, wide(m), ALU.subtract), base)
                link(nc.vector.tensor_tensor(sq_, xc, xc, ALU.mult), base)
                nc.vector.tensor_reduce(var, sq_, AX.X, ALU.add).then_inc(var_sem, 1)
                dve.wait_ge(std_sem, var_value)
                link(nc.vector.reciprocal(r, std), base)
                link(nc.vector.tensor_scalar(m, var, 1.0 / D, EPS, ALU.mult, ALU.add), base)
                link(nc.vector.tensor_tensor(e, r, r, ALU.mult), base)
                link(nc.vector.tensor_tensor(e, e, m, ALU.mult), base)
                link(nc.vector.tensor_scalar(e, e, -0.5, 1.5, ALU.mult, ALU.add), base)
                link(nc.vector.tensor_tensor(r, r, e, ALU.mult), base)
                return nc.vector.scalar_tensor_tensor(h_out, xc, 0.0, wide(r), ALU.max, ALU.mult)

            nc.vector.memset(zeros[:, :], 0.0).then_inc(zero_ready, 1)
            link(nc.vector.memset(epsb[:, :], EPS))
            link(nc.vector.memset(st[:, :, :], 0.0))
            for k in range(PRE):
                a, b = k * PT, (k + 1) * PT
                u3 = U_[:, :].rearrange("p (t d) -> p t d", d=D)
                s3 = sq[:, :].rearrange("p (t d) -> p t d", d=D)
                dve.wait_ge(x_in[k], 16)
                link(norm(X[:, a:b, :], H[:, a:b, 0:D], s3, PT, a, 0, pre_var, k + 1, pre_std, H[:, a:b, 0:D], None))
                dve.wait_ge(u_in[k], 16)
                link(nc.vector.tensor_scalar(s3, u3, float(np.float32(P_DROP)), float(np.float32(1.0) / np.float32(1.0 - P_DROP)),
                                             ALU.is_ge, ALU.mult))
                dve.sem_inc(u_used, 1)
                nc.vector.tensor_tensor(H[:, a:b, 0:D], H[:, a:b, 0:D], s3, ALU.mult).then_inc(h0_ready, 1)

            dve.wait_ge(h0_ready, PRE)
            base0 = count[0]
            per_row = 12
            with dve.Fori(0, NB) as i:
                count[0] = 0
                base = base0 + per_row * i
                dve.wait_ge(a_done, i + 1)
                dve.wait_ge(a_part, i + 1)
                nc.vector.tensor_copy(fus, psF[:, :]).then_inc(a_f_out, 1)
                dve.wait_ge(a_xp, i + 1)
                rows = X[:, bass.ds(Q * i, Q), :]
                link(nc.vector.tensor_tensor(xs[:, :, :], psZ[:, :].rearrange("p (q d) -> p q d", d=D), rows, ALU.add), base)
                link(norm(xs[:, :, :], xc[:, :, :], h2s[:, :, :], Q, 0, base, a_var, i + 1, a_std,
                          H[:, bass.ds(Q * i, Q), D:2 * D], None), base)
                settle(dve)
                nc.vector.tensor_copy(rows, xs[:, :, :]).then_inc(a_h1, 1)
                assert count[0] == per_row
            base0 += per_row * NB

            dve.wait_ge(a_h1, NB)
            dve.wait_ge(a_part, NB + 1)
            dve.sem_inc(b_fout, 1)
            dve.sem_inc(b_h2, 1)
            dve.sem_inc(b_added, 2)
            high = cat[D:P, :].unsqueeze(1)

            def end_row_b(t, first=False):
                own = bass.ds(NB - 1 - t, 1)
                dve.wait_ge(b_done, t + 1)
                settle(dve)
                nc.vector.tensor_tensor(high, psF[D:P, :].unsqueeze(1), part[D:P, own, :], ALU.add).then_inc(b_up, 1)
                nc.vector.tensor_copy(part[0:D, own, :], psF[0:D, :].unsqueeze(1)).then_inc(b_fout, 1)
                dve.wait_ge(b_up, t + 1)
                dve.wait_ge(b_d1, t + 1)
                nc.vector.tensor_tensor(high, psD1[D:P, :].unsqueeze(1), high, ALU.add).then_inc(b_cat, 1)
                if first:
                    dve.sem_inc(b_d3out, 1)
                else:
                    dve.wait_ge(b_d3, t + 1)
                    dve.wait_ge(b_fout, t + 1)
                    settle(dve)
                    before = bass.ds(NB - t, 1)
                    lo = part[0:D, before, :]
                    nc.vector.tensor_tensor(lo, psD3[0:D, :].unsqueeze(1), lo, ALU.add)
                    nc.vector.tensor_copy(part[D:P, before, :], psD3[D:P, :].unsqueeze(1)).then_inc(b_d3out, 1)
                dve.wait_ge(b_h2s, t + 1)
                settle(dve)
                nc.vector.tensor_copy(H[:, bass.ds(Q * (NB - 1) - Q * t, Q), 0:D], h2s[:, :, :]).then_inc(b_h2, 1)

            end_row_b(0, True)
            for a in range(SETS):
                with dve.Fori(0, rows_in(a)) as b:
                    for q in range(a + 1):
                        for k in range(ITEMS):
                            s = ITEMS * q + k
                            item = ITEMS * (fours(a, b) + q) + k

                            def add():
                                dve.wait_ge(b_under, item + 1)
                                dve.wait_ge(b_added, item + 1)
                                nc.vector.tensor_tensor(part[:, NB - 1 - s, :], (psU, psV)[k % 2][:, :],
                                                        part[:, NB - 1 - s, :], ALU.add).then_inc(b_added, 1)

                            def no_add():
                                dve.wait_ge(b_under, item + 1)
                                dve.sem_inc(b_added, 1)

                            under(dve, b, a, q, k, add, no_add)
                    end_row_b(b + ITEMS * a + 1)

            dve.sem_inc(e_cat, 2)
            dve.sem_inc(e_o, 1)
            dve.wait_ge(b_added, 2 + ITEMS * ALL_FOURS)

            def sum_tail(r, k):
                dve.wait_ge(e_mm, r + 1)
                settle(dve)
                nc.vector.tensor_tensor(cat2[:, k % 2, :].unsqueeze(1), (psU, psV)[k % 2][:, :].unsqueeze(1),
                                        part[:, bass.ds(NB - 1 - r, 1), :], ALU.add).then_inc(e_cat, 1)

            def out_tail(r):
                dve.wait_ge(e_th, r + 2)
                settle(dve)
                rows = X[:, bass.ds(Q * (NB - 1) - Q * r, Q), :]
                nc.vector.tensor_tensor(rows, xs[:, :, :], rows, ALU.add).then_inc(e_o, 1)

            sum_tail(0, 0)
            dve.wait_ge(b_d3, NB + 1)
            nc.vector.tensor_tensor(part[0:D, 0, :], psD3[0:D, :], part[0:D, 0, :], ALU.add)
            nc.vector.tensor_copy(part[D:P, 0, :], psD3[D:P, :]).then_inc(b_d3out, 1)
            with dve.Fori(0, 7) as c:
                for k in range(1, 3):
                    r = 2 * c + k
                    sum_tail(r, k)
                    out_tail(r - 1)
            dve.wait_ge(b_d3out, NB + 1)
            dve.wait_ge(e_z, 14)
            nc.vector.tensor_copy(cat2[:, 1, :], part[:, 0, :]).then_inc(e_cat, 1)
            out_tail(14)
            out_tail(15)

        @block.gpsimd
        def _(pool):
            pool.sem_inc(a_part, 1)
            with pool.Fori(0, NB) as i:
                pool.wait_ge(a_f_out, i + 1)
                settle(pool)
                nc.gpsimd.tensor_copy(part[D:P, bass.ds(i, 1), :], fus[D:P, :].unsqueeze(1)).then_inc(a_part, 1)

            pool.wait_ge(a_part, NB + 1)
            pool.wait_ge(a_h1, NB)
            nc.gpsimd.tensor_copy(hs[:, :, :], H[:, Q * (NB - 1):, D:2 * D]).then_inc(b_hs, 1)

            def h2_of_column(a, b):
                first = nc.s_assert_within(Q * (NB - ITEMS * a) - Q * b, 0, Q * (NB - 1),
                                           skip_runtime_bounds_check_because="only rows with b > 1 get here where a is 0")
                pool.wait_ge(b_under, ITEMS * fours(a, b))
                pool.wait_ge(b_h2, b + ITEMS * a + 1)
                settle(pool)
                nc.gpsimd.tensor_copy(col[:, :, :], H[:, bass.ds(first, Q), 0:D]).then_inc(b_col, 1)

            for a in range(SETS):
                with pool.Fori(0, rows_in(a)) as b:
                    t = b + ITEMS * a + 1
                    pool.wait_ge(b_d1, t)
                    settle(pool)
                    nc.gpsimd.tensor_copy(hs[:, :, :], H[:, bass.ds(Q * (NB - 1) - Q * t, Q), D:2 * D]).then_inc(b_hs, 1)
                    if a:
                        h2_of_column(a, b)
                    else:
                        with pool.If(b > 1):
                            h2_of_column(a, b)
                        with pool.Else():
                            pool.sem_inc(b_col, 1)

            def h2_of(r):
                nc.gpsimd.tensor_copy(hs[:, :, :], H[:, bass.ds(Q * (NB - 1) - Q * r, Q), 0:D]).then_inc(e_hs, 1)

            def store(r):
                pool.wait_ge(e_o, r + 2)
                settle(pool)
                pool.dma_start(out[NB - 1 - r], X[:, bass.ds(Q * (NB - 1) - Q * r, Q), :]
                               .rearrange("p q d -> p (q d)")).then_inc(e_out, 16)

            pool.wait_ge(b_d1, NB)
            nc.gpsimd.tensor_copy(hs[:, :, :], H[:, Q * (NB - 1):, 0:D]).then_inc(e_hs, 1)
            pool.wait_ge(b_h2, NB + 1)
            with pool.Fori(1, NB) as r:
                pool.wait_ge(e_T, r + 1)
                settle(pool)
                h2_of(r)
                store(r - 1)
            pool.wait_ge(e_o, NB + 1)
            pool.dma_start(out[0], X[:, 0:Q, :].rearrange("p q d -> p (q d)")).then_inc(e_out, 16)
            pool.wait_ge(e_out, 16 * NB)


def kernel(x, adj, L0_gnn_u, L1_gnn_W):
    import concourse.bacc as bacc
    from concourse.bass_utils import run_bass_kernel_spmd

    def tiles(a):
        return np.ascontiguousarray(np.asarray(a).reshape(KT, P, D).transpose(1, 0, 2)).reshape(P, KT * D)

    blocks = np.asarray(adj).reshape(NB, BLK, NB, Q, P).transpose(0, 2, 4, 3, 1)
    arrays = {
        "adj": np.ascontiguousarray(blocks).reshape(NB * NB, P, Q * BLK),
        "x": tiles(x),
        "u": tiles(L0_gnn_u),
        "w": np.ascontiguousarray(L1_gnn_W),
        "eye": np.eye(P, dtype=np.float32),
    }
    nc = bacc.Bacc("TRN2", target_bir_lowering=False, num_devices=1)
    ins = {k: nc.dram_tensor(f"{k}_dram", a.shape, F32, kind="ExternalInput").ap() for k, a in arrays.items()}
    out = nc.dram_tensor("out_dram", (NB, P, Q * D), F32, kind="ExternalOutput").ap()
    gnn_program(nc, ins["adj"], ins["x"], ins["u"], ins["w"], ins["eye"], out)
    r = run_bass_kernel_spmd(nc, [{f"{k}_dram": a for k, a in arrays.items()}], core_ids=[0])
    got = r.results[0]["out_dram"]
    return np.asarray(got).reshape(NB, P, Q, D).transpose(0, 2, 1, 3).reshape(N, D)
```

```python
from contextlib import ExitStack

import numpy as np
import concourse.bass as bass
from concourse import mybir

N, D = 8192, 64
P = 128
BLK = 512
NB = N // BLK
Q = BLK // P
KT = N // P
SLOTS = 8
USES = NB // SLOTS
ITEMS = SLOTS // 2
SETS = range(1, NB // ITEMS)
SHORT = range(1, ITEMS + 1)
KEPT = {s: NB - 1 if s < 2 else s for s in (0, 1, *range(NB - ITEMS, NB))}
LATE = (NB - 3, NB - 2)
AHEAD = (1, 2, 3)
PIECES = [1, 3, 4, 4, 4]
EPS = 1e-5
P_DROP = 0.1

F32 = mybir.dt.float32
BF16 = mybir.dt.bfloat16
ALU = mybir.AluOpType
ACT = mybir.ActivationFunctionType
AX = mybir.AxisListType


def rows_in(a):
    return ITEMS if a < SETS[-1] else ITEMS - 1


def fours_before(a):
    return sum(rows_in(c) * (c + 1) for c in SETS if c < a)


def short_row(t):
    place = sum(2 * r - 2 if r > 2 else r for r in SHORT if r < t)
    number = sum(r - 2 for r in SHORT if 2 < r < t)
    for s0 in range(0, t, 2):
        pair = range(s0, min(s0 + 2, t))
        for s in pair:
            yield False, s, 0, place, None
            place += 1
        for s in pair:
            if s < t - 2:
                yield True, s, 0, place, number
                place += 1
                number += 1


SHORT_BLOCKS = 1 + max(x[3] for t in SHORT for x in short_row(t))
SHORT_UNDER = 1 + max(x[4] for t in SHORT for x in short_row(t) if x[0])


def long_row(a):
    for q in range(a + 1):
        before = SHORT_BLOCKS + SLOTS * (fours_before(a) + q)
        turn = 2 if q == a else 0
        for k0 in range(0, ITEMS, 2):
            place = [before + (2 * k0 + n + turn) % SLOTS for n in range(4)]
            for k in (k0, k0 + 1):
                yield False, ITEMS * q + k, max(0, k - ITEMS * (a - q)), place[k - k0], None
            for k in (k0, k0 + 1):
                yield (True, ITEMS * q + k, max(0, k + 2 - ITEMS * (a - q)), place[2 + k - k0],
                       SHORT_UNDER + ITEMS * (fours_before(a) + q) + k)


B_BLOCKS = SHORT_BLOCKS + SLOTS * fours_before(SETS[-1] + 1)
B_UNDER = SHORT_UNDER + ITEMS * fours_before(SETS[-1] + 1)


def diag_buffer(t):
    return 2 + t if t < 2 else t % 2


def row_at(r):
    return (0, 1)[r - (NB - 2)] if isinstance(r, int) and r >= NB - 2 else NB - 1 - r


def tiles_at(r):
    return bass.ds(Q * row_at(r), Q) if isinstance(r, int) else bass.ds(Q * (NB - 1) - Q * r, Q)


def gnn_program(nc, adj, x, u, w, eye, out):
    with ExitStack() as ctx:
        def sb(name, shape, dt=F32):
            return ctx.enter_context(nc.sbuf_tensor(name, shape, dt))

        def bank(name, shape):
            return ctx.enter_context(nc.psum_tensor(name, shape, F32))

        def sem(name):
            return ctx.enter_context(nc.semaphore(name))

        ring = sb("ring", [P, SLOTS, Q * BLK])
        diag = sb("diag", [P, 4, Q * BLK])
        spare = sb("spare", [P, 2, Q * BLK])
        early = [spare[:, 1, :], spare[:, 0, :], diag[:, 2, :], diag[:, 3, :]]
        H = sb("H", [P, KT, 2 * D])
        X = sb("X", [P, KT, D])
        part = sb("part", [P, NB, BLK])
        per = BLK // D
        U_ = part[:, 0:KT // per, :].rearrange("p i (t d) -> p (i t) d", d=D)
        scratch = part[:, KT // per:KT // per + 2, :].rearrange("p i (t d) -> p (i t) d", d=D)
        cat2 = sb("cat2", [P, 2, BLK])
        cat = cat2[:, 0, :]
        fus = sb("fus", [P, BLK])
        low = sb("low", [P, BLK])
        first = low
        hs = sb("hs", [P, Q, D])
        h2s = sb("h2s", [P, Q, D])
        xs = sb("xs", [P, Q, D])
        col = sb("col", [P, Q, D])
        xc = col
        ident = sb("ident", [P, P])
        eye2 = sb("eye2", [P, D])
        ws = sb("ws", [P, 2, D])
        zeros = sb("zeros", [P, BLK], BF16)
        epsb = sb("epsb", [P, 1])
        st = sb("st", [P, 6, KT])

        psU = bank("psU", [P, BLK])
        psF = bank("psF", [P, BLK])
        psV = bank("psV", [P, BLK])
        psD1 = bank("psD1", [P, BLK])
        psD3 = bank("psD3", [P, BLK])
        psT = bank("psT", [D, BLK])
        psZ = bank("psZ", [P, Q * D])

        slot_full = [sem(f"slot_full{k}") for k in range(SLOTS)]
        slot_free = [sem(f"slot_free{k}") for k in range(SLOTS)]
        diag_first = [sem(f"diag_first{t}") for t in range(ITEMS)]
        early_full = [sem(f"early_full{k}") for k in range(len(early))]
        diag_full, consts = sem("diag_full"), sem("consts")
        x_in = [sem(f"x_in{k}") for k in range(len(PIECES))]
        u_in = [sem(f"u_in{k}") for k in range(len(PIECES))]
        h0_ready, pre_var, pre_std = sem("h0_ready"), sem("pre_var"), sem("pre_std")
        zero_ready = sem("zero_ready")
        dchain, settled = sem("dchain"), sem("settled")
        a_v_done, a_v_out = sem("a_v_done"), sem("a_v_out")
        a_done, a_u_out, a_f_out, a_part, a_xp = [sem(n) for n in ("a_done", "a_u_out", "a_f_out", "a_part", "a_xp")]
        a_var, a_std, a_h1 = sem("a_var"), sem("a_std"), sem("a_h1")
        b_ahead = sem("b_ahead")
        b_hs, b_d1, b_T, b_hT, b_low, b_done, b_up, b_cat, b_fout = [sem(n) for n in (
            "b_hs", "b_d1", "b_T", "b_hT", "b_low", "b_done", "b_up", "b_cat", "b_fout")]
        b_z, b_h2s, b_h2, b_d3, b_d3out = [sem(n) for n in ("b_z", "b_h2s", "b_h2", "b_d3", "b_d3out")]
        b_col, b_under, b_added = sem("b_col"), sem("b_under"), sem("b_added")
        e_hs, e_T, e_hT, e_mm, e_sum, e_low, e_cat, e_z, e_th, e_o, e_out, e_last = [sem(n) for n in (
            "e_hs", "e_T", "e_hT", "e_mm", "e_sum", "e_low", "e_cat", "e_z", "e_th", "e_o", "e_out", "e_last")]

        block = ctx.enter_context(nc.Block())

        def settle(eng):
            eng.sem_inc(settled, 1)

        def slot(s):
            return ring[:, s % SLOTS, :]

        def bank_d1(t):
            return {1: psV, 2: psU}[t] if isinstance(t, int) and t in (1, 2) else psD1

        def kept(s):
            return spare[:, s, :] if s < 2 else diag[:, diag_buffer(NB - 1 - s), :]

        def kept_full(s):
            return early_full[1 - s] if s < 2 else diag_first[NB - 1 - s]

        def among(eng, b, a, least, then, otherwise):
            if least == 0:
                then()
            elif least >= rows_in(a):
                otherwise()
            else:
                with eng.If(b > least - 1):
                    then()
                with eng.Else():
                    otherwise()

        def slot_use(place, a=None, b=None):
            use = USES * NB + place // SLOTS
            return place % SLOTS, use if a is None else use + (a + 1) * b

        def number_of(number, a=None, b=None):
            return number if a is None else number + ITEMS * (a + 1) * b

        @block.sync
        def _(sp):
            last = 0
            for k, blocks in enumerate(PIECES):
                lo, hi = Q * last, Q * (last + blocks)
                sp.dma_start(X[:, lo:hi, :], x[:, lo * D:hi * D]).then_inc(x_in[k], 16)
                sp.dma_start(U_[:, lo:hi, :], u[:, lo * D:hi * D]).then_inc(u_in[k], 16)
                for s in range(last, min(last + blocks, SLOTS)):
                    sp.dma_start(slot(s), adj[s]).then_inc(slot_full[s], 16)
                last += blocks
            for s in range(SLOTS, NB):
                sp.wait_ge(slot_free[s % SLOTS], s // SLOTS)
                sp.dma_start(slot(s), adj[s]).then_inc(slot_full[s % SLOTS], 16)
            with sp.Fori(1, NB) as i:
                for s in range(NB):
                    sp.wait_ge(slot_free[s % SLOTS], USES * i + s // SLOTS)
                    if s in KEPT:
                        settle(sp)
                        with sp.If(i == KEPT[s]):
                            sp.dma_start(kept(s), adj[KEPT[s] * NB + s]).then_inc(kept_full(s), 16)
                            sp.sem_inc(slot_full[s % SLOTS], 16)
                        with sp.Else():
                            sp.dma_start(slot(s), adj[i * NB + s]).then_inc(slot_full[s % SLOTS], 16)
                    else:
                        sp.dma_start(slot(s), adj[i * NB + s]).then_inc(slot_full[s % SLOTS], 16)

            def load(k, use, block):
                sp.wait_ge(slot_free[k], use)
                settle(sp)
                sp.dma_start(ring[:, k, :], block()).then_inc(slot_full[k], 16)

            def skip(k):
                sp.sem_inc(slot_free[k], 1)

            for t in SHORT:
                for is_under, s, _, place, _ in short_row(t):
                    m, use = slot_use(place)
                    block_at = NB * (NB - 1 - s) + NB + 1 - t if is_under else NB * (NB - 1 - t) + NB - 1 - s
                    sp.wait_ge(slot_free[m], use)
                    sp.dma_start(ring[:, m, :], adj[block_at]).then_inc(slot_full[m], 16)
                if t >= ITEMS:
                    sp.wait_ge(b_d3, t)
                    sp.dma_start(diag[:, diag_buffer(t), :], adj[(NB + 1) * (NB - 1 - t)]).then_inc(diag_full, 16)
            for k in (2, 3):
                sp.dma_start(early[k], adj[NB * (NB - 1 - k // 2) + 1 - k % 2]).then_inc(early_full[k], 16)
            for a in SETS:
                with sp.Fori(0, rows_in(a)) as b:
                    for is_under, s, least, place, _ in long_row(a):
                        m, use = slot_use(place, a, b)
                        among(sp, b, a, least,
                              lambda: load(m, use, lambda: adj[
                                  NB * (NB - 1 - s) + NB - ITEMS * a - b if is_under else
                                  NB * NB - 1 - s - NB * (ITEMS * a + 1) - NB * b]),
                              lambda: skip(m))
                    sp.wait_ge(b_d3, ITEMS * a + 1 + b)
                    settle(sp)
                    where = NB * NB - 1 - (NB + 1) * (ITEMS * a + 1) - (NB + 1) * b
                    with sp.If(b % 2 == 0):
                        sp.dma_start(diag[:, 1, :], adj[where]).then_inc(diag_full, 16)
                    with sp.Else():
                        sp.dma_start(diag[:, 0, :], adj[where]).then_inc(diag_full, 16)

            def load_tail(r, j, c, row):
                m, use = slot_use(B_BLOCKS + 2 * (r - 2) + j)
                load(m, use + c, lambda: adj[NB * row + 1 - j])

            with sp.Fori(0, 3) as c:
                for k in range(2, 2 + ITEMS):
                    for j in range(2):
                        load_tail(k, j, c, NB - 1 - k - ITEMS * c)
            m, use = slot_use(B_BLOCKS + 24)
            sp.wait_ge(slot_free[m], use)
            sp.dma_start(ring[:, m, :], adj[NB]).then_inc(slot_full[m], 16)
            for r in (14, 15):
                sp.wait_ge(e_o, r + 2)
                sp.dma_start(out[row_at(r)], X[:, tiles_at(r), :]
                             .rearrange("p q d -> p (q d)")).then_inc(e_last, 16)
            sp.wait_ge(e_last, 16 * 2)

        @block.tensor
        def _(pe):
            def open_bank(ps):
                nc.tensor.matmul(ps[:, :], zeros[:, 0:P], zeros[:, :], start=True, stop=False, skip_group_check=True)

            def one(ps, moving, h, start=False):
                for q in range(Q):
                    lo = D * (q % 2)
                    m = nc.tensor.matmul(ps[lo:lo + D, :], h(q), moving[:, q * BLK:(q + 1) * BLK],
                                         start=start and q < 2, stop=q >= Q - 2, skip_group_check=True)
                return m

            def two(ps, moving, h, start=False):
                for q in range(Q):
                    m = nc.tensor.matmul(ps[:, :], h(q), moving[:, q * BLK:(q + 1) * BLK],
                                         start=start and q == 0, stop=q == Q - 1, skip_group_check=True)
                return m

            def left(j):
                return lambda q: H[:, Q * j + q, 0:D]

            def both(j):
                return lambda q: H[:, Q * j + q, :]

            def first_layer_rows():
                for q in range(Q):
                    m = nc.tensor.matmul(psZ[:, q * D:(q + 1) * D], cat[:, q * P:(q + 1) * P], eye2[:, :],
                                         start=True, stop=True)
                m.then_inc(a_xp, 1)

            def transposes(src):
                for q in range(Q):
                    m = nc.tensor.transpose(psT[:, q * P:(q + 1) * P], src[:, q, :], ident[:, :])
                return m

            def weights(hop, cat=cat):
                for q in range(Q):
                    m = nc.tensor.matmul(psZ[:, q * D:(q + 1) * D], cat[:, q * P:(q + 1) * P], ws[:, hop, :],
                                         start=True, stop=True)
                return m

            pe.wait_ge(zero_ready, 1)

            def row_a(i, first):
                if first:
                    open_bank(psU)
                    open_bank(psF)
                    open_bank(psV)
                else:
                    with pe.If(i < 2):
                        pe.wait_ge(a_u_out, 2 * i)
                        settle(pe)
                        first_layer_rows()
                    pe.wait_ge(slot_full[0], 16 * USES * i + 16)
                    pe.wait_ge(a_h1, 1)
                    pe.wait_ge(a_v_out, i)
                    with pe.If(i == KEPT[0]):
                        pe.wait_ge(kept_full(0), 16)
                        two(psV, kept(0), both(0), start=True).then_inc(slot_free[0], 1)
                    with pe.Else():
                        two(psV, slot(0), both(0), start=True).then_inc(slot_free[0], 1)
                    with pe.If(i > 1):
                        pe.wait_ge(a_u_out, 2 * i)
                        settle(pe)
                        first_layer_rows()
                    pe.wait_ge(a_u_out, 2 * i)
                    pe.wait_ge(a_f_out, i + 1)
                    open_bank(psU)
                    with pe.If(i < 2):
                        open_bank(psF)
                nc.tensor.matmul(psV[:, 0:1], zeros[:, 0:P], zeros[:, 0:1], start=False, stop=True,
                                 skip_group_check=True).then_inc(a_v_done, 1)
                for s in range(0 if first else 1, NB):
                    if first:
                        pe.wait_ge(h0_ready, 1 + sum(s >= sum(PIECES[:k + 1]) for k in range(len(PIECES))))
                        pe.wait_ge(slot_full[s % SLOTS], 16 * (s // SLOTS + 1))
                        one(psU, slot(s), left(s)).then_inc(slot_free[s % SLOTS], 1)
                        continue
                    pe.wait_ge(slot_full[s % SLOTS], 16 * (USES * i + s // SLOTS + 1))

                    def single():
                        one(psU, slot(s), left(s)).then_inc(slot_free[s % SLOTS], 1)

                    def single_kept():
                        pe.wait_ge(kept_full(s), 16)
                        one(psU, kept(s), left(s)).then_inc(slot_free[s % SLOTS], 1)

                    def fused():
                        pe.wait_ge(a_h1, s + 1)
                        two(psF, slot(s), both(s), start=s == 1).then_inc(slot_free[s % SLOTS], 1)

                    def fused_kept():
                        pe.wait_ge(a_h1, s + 1)
                        pe.wait_ge(kept_full(s), 16)
                        two(psF, kept(s), both(s), start=s == 1).then_inc(slot_free[s % SLOTS], 1)

                    def single_late():
                        one(psU, slot(s), left(s))

                    with pe.If(i < s + 1):
                        if KEPT.get(s) == s:
                            with pe.If(i == s):
                                single_kept()
                            with pe.Else():
                                single()
                        else:
                            single()
                    with pe.Else():
                        if s in KEPT and KEPT[s] > s:
                            with pe.If(i == KEPT[s]):
                                fused_kept()
                            with pe.Else():
                                fused()
                        elif s in LATE:
                            with pe.If(i == NB - 1):
                                single_late()
                            with pe.Else():
                                fused()
                        else:
                            fused()
                nc.tensor.matmul(psU[:, 0:1], zeros[:, 0:P], zeros[:, 0:1], start=False, stop=True,
                                 skip_group_check=True).then_inc(a_done, 1)

            row_a(0, True)
            pe.wait_ge(consts, 16 * 5)
            with pe.Fori(1, NB) as i:
                row_a(i, False)

            def right_half(j):
                return lambda q: H[:, Q * j + q, D:2 * D]

            def ahead(t):
                pe.wait_ge(diag_first[t], 16)
                pe.wait_ge(a_h1, NB - t)
                one(bank_d1(t), diag[:, diag_buffer(t), :], right_half(NB - 1 - t), start=True).then_inc(b_ahead, 1)

            pe.wait_ge(a_v_out, NB)
            ahead(1)
            pe.wait_ge(a_u_out, 2 * NB)
            first_layer_rows()
            for s in LATE:
                pe.wait_ge(a_h1, s + 1)
                one(psD1, slot(s), right_half(s), start=s == LATE[0]).then_inc(slot_free[s % SLOTS], 1)
            ahead(2)

            fixed = lambda h: lambda q: h[:, q, :]

            def row_b(t, a=None, b=None):
                pe.wait_ge(b_fout, t + 1)
                if a is None and t == 0:
                    open_bank(psF)
                pe.wait_ge(b_hs, t + 1)
                settle(pe)
                transposes(hs).then_inc(b_T, 1)
                rows = long_row(a) if a else short_row(t) if t else ()
                seen = False
                for is_under, s, least, place, number in rows:
                    m, use = slot_use(place, a, b)
                    full = 16 * use + 16

                    def right():
                        pe.wait_ge(slot_full[m], full)
                        pe.wait_ge(b_h2, s + 2)
                        two(psF, ring[:, m, :], both(NB - 1 - s), start=s == 0).then_inc(slot_free[m], 1)

                    def below():
                        if not seen:
                            pe.wait_ge(b_col, t - 2)
                        pe.wait_ge(slot_full[m], full)
                        pe.wait_ge(b_added, nth + 1)
                        ps = (psU, psV)[number % 2]
                        one(ps, ring[:, m, :], fixed(col), start=True).then_inc(slot_free[m], 1)
                        nc.tensor.matmul(ps[:, 0:1], zeros[:, 0:P], zeros[:, 0:1], start=False, stop=True,
                                         skip_group_check=True).then_inc(b_under, 1)

                    def none_below():
                        pe.wait_ge(b_added, nth + 2)
                        pe.sem_inc(b_under, 1)
                        pass_slot()

                    def pass_slot():
                        pe.sem_inc(slot_full[m], 16)

                    if is_under:
                        nth = number_of(number, a, b)
                        among(pe, b, a, least, below, none_below)
                        seen = seen or least == 0
                    else:
                        among(pe, b, a, least, right, pass_slot)
                nc.tensor.matmul(psF[:, 0:1], zeros[:, 0:P], zeros[:, 0:1], start=False, stop=True,
                                 skip_group_check=True).then_inc(b_done, 1)
                if a is None and t < ITEMS:
                    pe.wait_ge(diag_first[t], 16)
                else:
                    pe.wait_ge(diag_full, 16 * (t - ITEMS) + 16)
                if a is None:
                    if t in AHEAD:
                        pe.sem_inc(b_d1, 1)
                    else:
                        one(psD1, diag[:, diag_buffer(t), :], fixed(hs), start=t > 0).then_inc(b_d1, 1)
                    if t == 0:
                        pe.sem_inc(b_d3, 1)
                    else:
                        pe.wait_ge(b_d3out, t)
                        pe.wait_ge(b_h2, t + 1)
                        one(psD3, diag[:, diag_buffer(t - 1), :], fixed(h2s), start=True).then_inc(b_d3, 1)
                else:
                    for last, (ps, h, there) in enumerate(((psD1, hs, b_d1), (psD3, h2s, b_d3))):
                        if last:
                            pe.wait_ge(b_d3out, t)
                            pe.wait_ge(b_h2, t + 1)
                        with pe.If(b % 2 == 0):
                            one(ps, diag[:, 1 - last, :], fixed(h), start=True).then_inc(there, 1)
                        with pe.Else():
                            one(ps, diag[:, last, :], fixed(h), start=True).then_inc(there, 1)
                pe.wait_ge(b_cat, t + 1)
                pe.wait_ge(b_hT, t + 1)
                weights(0).then_inc(b_z, 1)
                if a is None and t == 0:
                    ahead(3)

            for t in (0, *SHORT):
                row_b(t)
            for a in SETS:
                with pe.Fori(0, rows_in(a)) as b:
                    row_b(b + ITEMS * a + 1, a, b)

            def row_tail(r, k, c):
                ps = (psU, psV)[k % 2]
                for j in range(2):
                    if k < 2:
                        block, freed = early[2 * k + j], None
                        pe.wait_ge(early_full[2 * k + j], 16)
                    else:
                        m, use = slot_use(B_BLOCKS + 2 * (k - 2) + j)
                        block, freed = ring[:, m, :], slot_free[m]
                        pe.wait_ge(slot_full[m], 16 * (use + c) + 16)
                    if j == 0:
                        pe.wait_ge(e_sum, r + 1)
                    else:
                        pe.wait_ge(b_h2, NB + 1)
                    for q in range(Q):
                        lo = D * (q % 2)
                        x = nc.tensor.matmul(ps[lo:lo + D, :], left(1 - j)(q), block[:, q * BLK:(q + 1) * BLK],
                                             start=j == 0 and q < 2, stop=j == 1 and q >= 2, skip_group_check=True)
                    if freed:
                        x.then_inc(freed, 1)
                nc.tensor.matmul(ps[:, 0:1], zeros[:, 0:P], zeros[:, 0:1], start=False, stop=True,
                                 skip_group_check=True).then_inc(e_mm, 1)

            def turn_tail(r):
                pe.wait_ge(e_hT, r + 1)
                pe.wait_ge(e_hs, r + 1)
                settle(pe)
                transposes(hs).then_inc(e_T, 1)

            def out_tail(r, k):
                pe.wait_ge(e_cat, r + 1)
                pe.wait_ge(e_hT, r + 2)
                pe.wait_ge(e_th, r + 1)
                settle(pe)
                weights(1, cat2[:, k % 2, :]).then_inc(e_z, 1)

            pe.sem_inc(e_T, 1)
            row_tail(0, 0, 0)
            turn_tail(0)
            pe.wait_ge(b_d3out, NB)
            one(psD3, diag[:, (NB - 1) % 2, :], fixed(h2s), start=True).then_inc(b_d3, 1)
            row_tail(1, 1, 0)
            turn_tail(1)
            out_tail(0, 0)
            with pe.Fori(0, 3) as c:
                for k in range(2, 2 + ITEMS):
                    r = ITEMS * c + k
                    row_tail(r, k, c)
                    turn_tail(r)
                    out_tail(r - 1, k - 1)
            m, use = slot_use(B_BLOCKS + 24)
            pe.wait_ge(slot_full[m], 16 * use + 16)
            pe.wait_ge(e_sum, 14 + 2)
            one(psV, ring[:, m, :], left(0), start=True).then_inc(slot_free[m], 1)
            nc.tensor.matmul(psV[:, 0:1], zeros[:, 0:P], zeros[:, 0:1], start=False, stop=True,
                             skip_group_check=True).then_inc(e_mm, 1)
            turn_tail(14)
            out_tail(13, 1)
            turn_tail(15)
            out_tail(14, 0)
            out_tail(15, 1)

        @block.scalar
        def _(act):
            act.dma_start(ident[:, :], eye).then_inc(consts, 16)
            act.dma_start(eye2[0:D, :], eye[0:D, 0:D]).then_inc(consts, 16)
            act.dma_start(eye2[D:P, :], eye[0:D, 0:D]).then_inc(consts, 16)
            act.dma_start(ws[0:D, :, :], w[:, D:2 * D, :].rearrange("k r c -> r k c")).then_inc(consts, 16)
            act.dma_start(ws[D:P, :, :], w[:, 0:D, :].rearrange("k r c -> r k c")).then_inc(consts, 16)
            last = 0
            for k, blocks in enumerate(PIECES):
                lo, hi = Q * last, Q * (last + blocks)
                last += blocks
                act.wait_ge(pre_var, k + 1)
                nc.scalar.activation(st[:, 2, lo:hi], st[:, 1, lo:hi],
                                     ACT.Sqrt, bias=epsb[:, 0:1], scale=1.0 / D).then_inc(pre_std, 1)
            with act.Fori(0, NB) as i:
                act.wait_ge(a_done, i + 1)
                nc.scalar.activation(cat[D:P, :], psU[D:P, :], ACT.Copy).then_inc(a_u_out, 1)
                act.wait_ge(a_var, i + 1)
                nc.scalar.activation(st[:, 2, 0:Q], st[:, 1, 0:Q], ACT.Sqrt, bias=epsb[:, 0:1],
                                     scale=1.0 / D).then_inc(a_std, 1)
            act.wait_ge(a_xp, NB)

            def row_b(t):
                act.wait_ge(b_T, t + 1)
                nc.scalar.activation(cat[0:D, :], psT[:, :], ACT.Copy).then_inc(b_hT, 1)
                if isinstance(t, int) and t in AHEAD:
                    act.wait_ge(b_ahead, t)
                    act.wait_ge(b_cat, t)
                else:
                    act.wait_ge(b_d1, t + 1)
                nc.scalar.activation(low[D:P, :], bank_d1(t)[0:D, :], ACT.Copy).then_inc(b_low, 1)
                act.wait_ge(b_h2, t + 1)
                act.wait_ge(b_d3, t + 1)
                act.wait_ge(b_z, t + 1)
                nc.scalar.activation(h2s[:, :, :], psZ[:, :].rearrange("p (q d) -> p q d", d=D),
                                     ACT.Tanh).then_inc(b_h2s, 1)

            for t in (0, *AHEAD):
                row_b(t)
            with act.Fori(AHEAD[-1] + 1, NB) as t:
                row_b(t)

            def turn_tail(r, k):
                act.wait_ge(e_T, r + 2)
                nc.scalar.activation(cat2[0:D, k % 2, :], psT[:, :], ACT.Copy).then_inc(e_hT, 1)

            def low_tail(r):
                act.wait_ge(e_sum, r + 3)
                nc.scalar.activation(low[D:P, :], fus[0:D, :], ACT.Copy).then_inc(e_low, 1)

            def out_tail(r):
                act.wait_ge(e_o, r + 1)
                act.wait_ge(e_z, r + 1)
                nc.scalar.activation(xs[:, :, :], psZ[:, :].rearrange("p (q d) -> p q d", d=D),
                                     ACT.Tanh).then_inc(e_th, 1)

            act.sem_inc(e_hT, 1)
            act.sem_inc(e_th, 1)
            low_tail(0)
            turn_tail(0, 0)
            with act.Fori(0, 6) as c:
                for k in range(1, 3):
                    r = 2 * c + k
                    low_tail(r)
                    turn_tail(r, k)
                    out_tail(r - 1)
            low_tail(13)
            turn_tail(13, 1)
            out_tail(12)
            act.wait_ge(b_d3out, NB + 1)
            act.wait_ge(e_cat, 14)
            nc.scalar.activation(low[D:P, :], part[0:D, 0, :], ACT.Copy).then_inc(e_low, 1)
            turn_tail(14, 0)
            out_tail(13)
            act.wait_ge(e_sum, 14 + 3)
            nc.scalar.activation(low[D:P, :], fus[0:D, :], ACT.Copy).then_inc(e_low, 1)
            turn_tail(15, 1)
            out_tail(14)
            out_tail(15)

        @block.vector
        def _(dve):
            count = [0]

            def link(ins, base=0):
                count[0] += 1
                ins.then_inc(dchain, 1)
                dve.wait_ge(dchain, base + count[0])

            def norm(xin, xc, sq_, n, k0, base, var_sem, var_value, std_sem, h_out):
                sum_, var, std, r, e, m = (st[:, j, k0:k0 + n] for j in range(6))
                wide = lambda a: a.unsqueeze(2).broadcast_to((P, n, D))
                link(nc.vector.tensor_reduce(sum_, xin, AX.X, ALU.add), base)
                link(nc.vector.tensor_scalar(m, sum_, 1.0 / D, None, ALU.mult), base)
                link(nc.vector.tensor_tensor(xc, xin, wide(m), ALU.subtract), base)
                link(nc.vector.tensor_tensor(sq_, xc, xc, ALU.mult), base)
                nc.vector.tensor_reduce(var, sq_, AX.X, ALU.add).then_inc(var_sem, 1)
                dve.wait_ge(std_sem, var_value)
                link(nc.vector.reciprocal(r, std), base)
                link(nc.vector.tensor_scalar(m, var, 1.0 / D, EPS, ALU.mult, ALU.add), base)
                link(nc.vector.tensor_tensor(e, r, r, ALU.mult), base)
                link(nc.vector.tensor_tensor(e, e, m, ALU.mult), base)
                link(nc.vector.tensor_scalar(e, e, -0.5, 1.5, ALU.mult, ALU.add), base)
                link(nc.vector.tensor_tensor(r, r, e, ALU.mult), base)
                return nc.vector.scalar_tensor_tensor(h_out, xc, 0.0, wide(r), ALU.max, ALU.mult)

            nc.vector.memset(zeros[:, :], 0.0).then_inc(zero_ready, 1)
            link(nc.vector.memset(epsb[:, :], EPS))
            link(nc.vector.memset(st[:, :, :], 0.0))
            last = 0
            for k, blocks in enumerate(PIECES):
                lo, hi = Q * last, Q * (last + blocks)
                last += blocks
                h0, s3 = H[:, lo:hi, 0:D], scratch[:, 0:hi - lo, :]
                dve.wait_ge(x_in[k], 16)
                link(norm(X[:, lo:hi, :], h0, s3, hi - lo, lo, 0, pre_var, k + 1, pre_std, h0))
                dve.wait_ge(u_in[k], 16)
                link(nc.vector.tensor_scalar(s3, U_[:, lo:hi, :], float(np.float32(P_DROP)),
                                             float(np.float32(1.0) / np.float32(1.0 - P_DROP)), ALU.is_ge, ALU.mult))
                nc.vector.tensor_tensor(h0, h0, s3, ALU.mult).then_inc(h0_ready, 1)

            dve.wait_ge(h0_ready, len(PIECES))
            base0 = count[0]
            per_row = 12
            dve.sem_inc(a_f_out, 1)
            with dve.Fori(0, NB) as i:
                count[0] = 0
                base = base0 + per_row * i
                dve.wait_ge(a_v_done, i + 1)
                dve.wait_ge(a_f_out, i + 1)
                nc.vector.tensor_copy(first[:, :], psV[:, :]).then_inc(a_v_out, 1)
                dve.wait_ge(a_done, i + 1)
                dve.wait_ge(a_part, i + 1)
                dve.wait_ge(a_v_out, i + 1)
                nc.vector.tensor_tensor(fus[:, :], psF[:, :], first[:, :], ALU.add).then_inc(a_f_out, 1)
                dve.wait_ge(a_f_out, i + 2)
                nc.vector.tensor_tensor(cat[0:D, :], psU[0:D, :], fus[0:D, :], ALU.add).then_inc(a_u_out, 1)
                dve.wait_ge(a_xp, i + 1)
                rows = X[:, bass.ds(Q * i, Q), :]
                link(nc.vector.tensor_tensor(xs[:, :, :], psZ[:, :].rearrange("p (q d) -> p q d", d=D), rows, ALU.add), base)
                link(norm(xs[:, :, :], xc[:, :, :], h2s[:, :, :], Q, 0, base, a_var, i + 1, a_std,
                          H[:, bass.ds(Q * i, Q), D:2 * D]), base)
                settle(dve)
                nc.vector.tensor_copy(rows, xs[:, :, :]).then_inc(a_h1, 1)
                assert count[0] == per_row
            base0 += per_row * NB

            dve.wait_ge(a_h1, NB)
            dve.wait_ge(a_part, NB + 1)
            dve.sem_inc(b_fout, 1)
            dve.sem_inc(b_h2, 1)
            dve.sem_inc(b_added, 2)
            high = cat[D:P, :].unsqueeze(1)

            def turn_sum(t):
                own = bass.ds(NB - 1 - t, 1)
                if isinstance(t, int) and t in AHEAD:
                    part1 = part[D:P, own, :]
                    dve.wait_ge(b_z, t)
                    dve.wait_ge(b_ahead, t)
                    nc.vector.tensor_tensor(high, bank_d1(t)[D:P, :].unsqueeze(1), part1, ALU.add).then_inc(b_up, 1)
                    dve.wait_ge(b_up, 2 * t + 1)
                    dve.wait_ge(b_low, t + 1)
                    nc.vector.tensor_tensor(high, low[D:P, :].unsqueeze(1), high, ALU.add).then_inc(b_up, 1)
                    dve.wait_ge(b_up, 2 * t + 2)
                    dve.wait_ge(b_done, t + 1)
                    nc.vector.tensor_tensor(high, psF[D:P, :].unsqueeze(1), high, ALU.add).then_inc(b_cat, 1)
                    nc.vector.tensor_copy(part[0:D, own, :], psF[0:D, :].unsqueeze(1)).then_inc(b_fout, 1)
                    return
                dve.wait_ge(b_done, t + 1)
                settle(dve)
                nc.vector.tensor_tensor(high, psF[D:P, :].unsqueeze(1), part[D:P, own, :], ALU.add).then_inc(b_up, 1)
                nc.vector.tensor_copy(part[0:D, own, :], psF[0:D, :].unsqueeze(1)).then_inc(b_fout, 1)
                dve.wait_ge(b_up, 2 * t + 1)
                dve.wait_ge(b_d1, t + 1)
                nc.vector.tensor_tensor(high, psD1[D:P, :].unsqueeze(1), high, ALU.add).then_inc(b_up, 1)
                dve.wait_ge(b_up, 2 * t + 2)
                dve.wait_ge(b_low, t + 1)
                nc.vector.tensor_tensor(high, low[D:P, :].unsqueeze(1), high, ALU.add).then_inc(b_cat, 1)

            def end_row_b(t):
                turn_sum(t)
                if isinstance(t, int) and t == 0:
                    dve.sem_inc(b_d3out, 1)
                else:
                    dve.wait_ge(b_d3, t + 1)
                    dve.wait_ge(b_fout, t + 1)
                    settle(dve)
                    before = bass.ds(NB - t, 1)
                    lo = part[0:D, before, :]
                    nc.vector.tensor_tensor(lo, psD3[0:D, :].unsqueeze(1), lo, ALU.add)
                    nc.vector.tensor_copy(part[D:P, before, :], psD3[D:P, :].unsqueeze(1)).then_inc(b_d3out, 1)
                dve.wait_ge(b_h2s, t + 1)
                settle(dve)
                nc.vector.tensor_copy(H[:, bass.ds(Q * (NB - 1) - Q * t, Q), 0:D], h2s[:, :, :]).then_inc(b_h2, 1)

            def sums(t, a=None, b=None):
                for is_under, s, least, _, number in long_row(a) if a else short_row(t):
                    if not is_under:
                        continue
                    nth = number_of(number, a, b)

                    def add():
                        dve.wait_ge(b_under, nth + 1)
                        dve.wait_ge(b_added, nth + 1)
                        nc.vector.tensor_tensor(part[:, NB - 1 - s, :], (psU, psV)[number % 2][:, :],
                                                part[:, NB - 1 - s, :], ALU.add).then_inc(b_added, 1)

                    def no_add():
                        dve.wait_ge(b_under, nth + 1)
                        dve.sem_inc(b_added, 1)

                    among(dve, b, a, least, add, no_add)

            end_row_b(0)
            for t in SHORT:
                sums(t)
                end_row_b(t)
            for a in SETS:
                with dve.Fori(0, rows_in(a)) as b:
                    t = b + ITEMS * a + 1
                    sums(t, a, b)
                    end_row_b(t)

            dve.sem_inc(e_sum, 2)
            dve.sem_inc(e_o, 1)
            dve.wait_ge(b_added, 2 + B_UNDER)

            def sum_tail(r, k):
                if not isinstance(r, int) or r > 0:
                    dve.wait_ge(e_cat, r)
                dve.wait_ge(e_mm, r + 1)
                settle(dve)
                nc.vector.tensor_tensor(fus[:, :].unsqueeze(1), (psU, psV)[k % 2][:, :].unsqueeze(1),
                                        part[:, bass.ds(NB - 1 - r, 1), :], ALU.add).then_inc(e_sum, 1)
                dve.wait_ge(e_sum, r + 3)
                dve.wait_ge(e_low, r + 1)
                nc.vector.tensor_tensor(cat2[D:P, k % 2, :], fus[D:P, :], low[D:P, :], ALU.add).then_inc(e_cat, 1)

            def out_tail(r):
                dve.wait_ge(e_th, r + 2)
                settle(dve)
                rows = X[:, tiles_at(r), :]
                nc.vector.tensor_tensor(rows, xs[:, :, :], rows, ALU.add).then_inc(e_o, 1)

            sum_tail(0, 0)
            dve.wait_ge(b_d3, NB + 1)
            nc.vector.tensor_tensor(part[0:D, 0, :], psD3[0:D, :], part[0:D, 0, :], ALU.add)
            nc.vector.tensor_copy(part[D:P, 0, :], psD3[D:P, :]).then_inc(b_d3out, 1)
            with dve.Fori(0, 6) as c:
                for k in range(1, 3):
                    r = 2 * c + k
                    sum_tail(r, k)
                    out_tail(r - 1)
            sum_tail(13, 1)
            out_tail(12)
            dve.wait_ge(b_d3out, NB + 1)
            dve.wait_ge(e_z, 13)
            dve.wait_ge(e_low, 15)
            nc.vector.tensor_tensor(cat2[D:P, 0, :], part[D:P, 0, :], low[D:P, :], ALU.add).then_inc(e_cat, 1)
            out_tail(13)
            dve.wait_ge(e_cat, 15)
            dve.wait_ge(e_mm, 15)
            nc.vector.tensor_tensor(fus[:, :], psV[:, :], part[:, 1, :], ALU.add).then_inc(e_sum, 1)
            dve.wait_ge(e_sum, 14 + 3)
            dve.wait_ge(e_low, NB)
            nc.vector.tensor_tensor(cat2[D:P, 1, :], fus[D:P, :], low[D:P, :], ALU.add).then_inc(e_cat, 1)
            out_tail(14)
            out_tail(15)

        @block.gpsimd
        def _(pool):
            pool.sem_inc(a_part, 1)
            with pool.Fori(0, NB) as i:
                pool.wait_ge(a_f_out, i + 2)
                settle(pool)
                nc.gpsimd.tensor_copy(part[D:P, bass.ds(i, 1), :], fus[D:P, :].unsqueeze(1)).then_inc(a_part, 1)

            pool.wait_ge(a_part, NB + 1)
            pool.wait_ge(a_h1, NB)
            nc.gpsimd.tensor_copy(hs[:, :, :], H[:, Q * (NB - 1):, D:2 * D]).then_inc(b_hs, 1)

            def row_b(t, seen):
                pool.wait_ge(b_T, t)
                pool.wait_ge(b_d1, t)
                settle(pool)
                nc.gpsimd.tensor_copy(hs[:, :, :], H[:, bass.ds(Q * (NB - 1) - Q * t, Q), D:2 * D]).then_inc(b_hs, 1)
                if seen is None:
                    return
                if not isinstance(seen, int) or seen > 0:
                    pool.wait_ge(b_under, seen)
                pool.wait_ge(b_h2, t)
                settle(pool)
                nc.gpsimd.tensor_copy(col[:, :, :], H[:, bass.ds(Q * (NB + 1) - Q * t, Q), 0:D]).then_inc(b_col, 1)

            for t in SHORT:
                row_b(t, next((number for is_under, _, _, _, number in short_row(t) if is_under), None))
            for a in SETS:
                with pool.Fori(0, rows_in(a)) as b:
                    row_b(b + ITEMS * a + 1, number_of(SHORT_UNDER + ITEMS * fours_before(a), a, b))

            def h2_of(r):
                pool.wait_ge(e_T, r + 1)
                settle(pool)
                nc.gpsimd.tensor_copy(hs[:, :, :], H[:, tiles_at(r), 0:D]).then_inc(e_hs, 1)

            def store(r):
                pool.wait_ge(e_o, r + 2)
                settle(pool)
                pool.dma_start(out[row_at(r)], X[:, tiles_at(r), :]
                               .rearrange("p q d -> p (q d)")).then_inc(e_out, 16)

            pool.wait_ge(b_d1, NB)
            nc.gpsimd.tensor_copy(hs[:, :, :], H[:, Q * (NB - 1):, 0:D]).then_inc(e_hs, 1)
            pool.wait_ge(b_h2, NB + 1)
            h2_of(1)
            with pool.Fori(2, NB - 2) as r:
                h2_of(r)
                store(r - 2)
            for r in (14, 15):
                h2_of(r)
                store(r - 2)
            pool.wait_ge(e_out, 16 * (NB - 2))


def kernel(x, adj, L0_gnn_u, L1_gnn_W):
    import concourse.bacc as bacc
    from concourse.bass_utils import run_bass_kernel_spmd

    def tiles(a):
        return np.ascontiguousarray(np.asarray(a).reshape(KT, P, D).transpose(1, 0, 2)).reshape(P, KT * D)

    blocks = np.asarray(adj).reshape(NB, BLK, NB, Q, P).transpose(0, 2, 4, 3, 1)
    arrays = {
        "adj": np.ascontiguousarray(blocks).reshape(NB * NB, P, Q * BLK),
        "x": tiles(x),
        "u": tiles(L0_gnn_u),
        "w": np.ascontiguousarray(L1_gnn_W),
        "eye": np.eye(P, dtype=np.float32),
    }
    nc = bacc.Bacc("TRN2", target_bir_lowering=False, num_devices=1)
    ins = {k: nc.dram_tensor(f"{k}_dram", a.shape, F32, kind="ExternalInput").ap() for k, a in arrays.items()}
    out = nc.dram_tensor("out_dram", (NB, P, Q * D), F32, kind="ExternalOutput").ap()
    gnn_program(nc, ins["adj"], ins["x"], ins["u"], ins["w"], ins["eye"], out)
    r = run_bass_kernel_spmd(nc, [{f"{k}_dram": a for k, a in arrays.items()}], core_ids=[0])
    got = r.results[0]["out_dram"]
    return np.asarray(got).reshape(NB, P, Q, D).transpose(0, 2, 1, 3).reshape(N, D)
```
